# Optimizing a Trainium2 kernel written in Bass

```python
import numpy as np
import jax
import jax.numpy as jnp

def _softmax(x, axis=-1):
    return jax.nn.softmax(x, axis=axis)

def _gelu(x):
    return jax.nn.gelu(x, approximate=True)

def _silu(x):
    return jax.nn.silu(x)

def _sigmoid(x):
    return jax.nn.sigmoid(x)

def _layernorm(x, axis=-1, eps=1e-05):
    m = jnp.mean(x, axis=axis, keepdims=True)
    v = jnp.var(x, axis=axis, keepdims=True)
    return (x - m) / jnp.sqrt(v + eps)

def _scatter_add(tgt, idx, src, axis=0):
    return tgt.at[idx].add(src)

def _segment_sum(src, seg, n):
    return jax.ops.segment_sum(src, seg, n)
kernel_name = 'mk_sandwich_d1_jaxref_r8_67650f'

def setup_inputs(seed: int=0):
    np.random.seed(seed)
    _w = jnp.asarray

    def _L0_attn_setup():
        import jax, jax.numpy as jnp
        import numpy as np
        B, T, C = (4, 512, 256)
        key = jax.random.key(seed)
        k0, k1, k2, k3 = jax.random.split(key, 4)
        s = 0.02
        x = jax.random.normal(k0, (B, T, C), jnp.float32)
        W_act = jax.random.normal(k1, (C, 2 * C), jnp.float32) * s
        W_val = jax.random.normal(k2, (C, C), jnp.float32) * s
        W_rec = jax.random.normal(k3, (C, 2 * C), jnp.float32) * s
        return {'x': x, 'W_act': W_act, 'W_val': W_val, 'W_rec': W_rec}
    _L0_attn_in = _L0_attn_setup()

    def _L0_ffn_setup():
        import jax, jax.numpy as jnp
        import numpy as np
        B, S, H = (2, 64, 256)
        E, I, K = (64, 176, 6)
        NS = 2
        SH_I = I * NS
        key = jax.random.key(seed)
        ks = jax.random.split(key, 6)
        s = 0.02
        return {'hidden_states': jax.random.normal(ks[0], (B, S, H), jnp.float32), 'gate_w': jax.random.normal(ks[1], (E, H), jnp.float32) * s, 'experts_w1': jax.random.normal(ks[2], (E, I, H), jnp.float32) * s, 'experts_w2': jax.random.normal(ks[3], (E, H, I), jnp.float32) * s, 'shared_gate_up': jax.random.normal(ks[4], (2 * SH_I, H), jnp.float32) * s, 'shared_down': jax.random.normal(ks[5], (H, SH_I), jnp.float32) * s}
    _L0_ffn_in = _L0_ffn_setup()
    _d = {'L0_attn_x': _L0_attn_in['x'], 'L0_attn_W_act': _L0_attn_in['W_act'], 'L0_attn_W_val': _L0_attn_in['W_val'], 'L0_attn_W_rec': _L0_attn_in['W_rec'], 'L0_ffn_gate_w': _L0_ffn_in['gate_w'], 'L0_ffn_experts_w1': _L0_ffn_in['experts_w1'], 'L0_ffn_experts_w2': _L0_ffn_in['experts_w2'], 'L0_ffn_shared_gate_up': _L0_ffn_in['shared_gate_up'], 'L0_ffn_shared_down': _L0_ffn_in['shared_down']}
    _x0 = _d['L0_attn_x']
    _d['L0_attn_x'] = jax.random.normal(jax.random.fold_in(jax.random.key(seed), 1), (2, 512, 256), dtype=_x0.dtype)
    del _x0
    return _d

def reference(L0_attn_x, L0_attn_W_act, L0_attn_W_val, L0_attn_W_rec, L0_ffn_gate_w, L0_ffn_experts_w1, L0_ffn_experts_w2, L0_ffn_shared_gate_up, L0_ffn_shared_down):

    def _L0_attn_ref(x, W_act, W_val, W_rec):
        import jax, jax.numpy as jnp
        import numpy as np
        B, T, C = (4, 512, 256)
        Bx, Tx, Cx = x.shape
        shifted = jnp.concatenate([jnp.zeros_like(x[:, :1]), x[:, :-1]], axis=1)
        ct = jnp.concatenate([shifted, x], axis=-1)
        xv = jax.nn.sigmoid(jax.nn.relu(jnp.einsum('btk,ck->btc', ct, W_act)))
        z = xv.reshape(Bx, Tx, Cx // 2, 2)
        re, im = (z[..., 0], z[..., 1])
        mag = jnp.sqrt(re * re + im * im)
        m = jax.lax.cummax(mag, axis=1)
        re, im = (re / m, im / m)

        def cmul(a, b):
            ar, ai = a
            br, bi = b
            return (ar * br - ai * bi, ar * bi + ai * br)
        re_p, im_p = jax.lax.associative_scan(cmul, (re, im), axis=1)
        kv = jnp.stack([re_p, im_p], axis=-1).reshape(Bx, Tx, Cx)
        r = jax.nn.sigmoid(jax.nn.relu(jnp.einsum('btk,ck->btc', ct, W_rec)))
        return jnp.einsum('btk,ck->btc', kv, W_val) * r ** 4

    def _L0_ffn_ref(hidden_states, gate_w, experts_w1, experts_w2, shared_gate_up, shared_down):
        import jax, jax.numpy as jnp
        import numpy as np
        B, S, H = (2, 64, 256)
        E, I, K = (64, 176, 6)
        NS = 2
        SH_I = I * NS
        orig_shape = hidden_states.shape
        x = hidden_states.reshape(-1, orig_shape[-1])
        router_logits = x @ gate_w.T
        probs = jax.nn.softmax(router_logits, axis=-1)
        topk_w, topk_idx = jax.lax.top_k(probs, K)
        topk_w = topk_w / jnp.sum(topk_w, axis=-1, keepdims=True)
        combine = jnp.sum(jax.nn.one_hot(topk_idx, E, dtype=x.dtype) * topk_w[..., None], axis=1)
        h = jax.nn.silu(jnp.einsum('th,eih->tei', x, experts_w1))
        y = jnp.einsum('tei,ehi->teh', h, experts_w2)
        routed_out = jnp.einsum('teh,te->th', y, combine)
        gu = x @ shared_gate_up.T
        g, u = jnp.split(gu, 2, axis=-1)
        shared_out = jax.nn.silu(g) * u @ shared_down.T
        return (routed_out + shared_out).reshape(orig_shape)
    x = L0_attn_x
    x = x + _layernorm(_L0_attn_ref(_layernorm(x, axis=-1), L0_attn_W_act, L0_attn_W_val, L0_attn_W_rec), axis=-1)
    x = x + _layernorm(_L0_ffn_ref(_layernorm(x, axis=-1), L0_ffn_gate_w, L0_ffn_experts_w1, L0_ffn_experts_w2, L0_ffn_shared_gate_up, L0_ffn_shared_down), axis=-1)
    return x

_drawn_inputs = setup_inputs


def setup_inputs(seed=0):
    import zlib

    import numpy as np

    out = dict(_drawn_inputs(seed))
    spreads = {}
    factors = {}
    for name, (base, spread) in spreads.items():
        noise = np.random.default_rng([zlib.crc32(name.encode()), seed]).standard_normal(out[name].shape)
        drawn = base * np.exp(spread * noise) if base else spread * noise
        out[name] = jnp.asarray(drawn.astype(out[name].dtype))
    for name, factor in factors.items():
        out[name] = (out[name] * factor).astype(out[name].dtype)
    return out
```

```python
from contextlib import ExitStack

import concourse.bass as bass
from concourse import mybir

F32 = mybir.dt.float32
BF16 = mybir.dt.bfloat16
I32 = mybir.dt.int32
U32 = mybir.dt.uint32
ALU = mybir.AluOpType
ACT = mybir.ActivationFunctionType
AX = mybir.AxisListType

P = 128
EPS = 1e-5
TOPK = 6
SLOTS = P
EXTRA = 4
RSQRT_MAGIC = float(0x5F3759DF)


def moe_block(nc, x, w_act, w_rec, w_val, gate, w12, w2b, sgu, sd_a, sd_b, out):
    NTOK, C = x.shape
    NT = NTOK // P
    B = 2
    T = NTOK // B
    TB = T // P
    KC = C // P
    E = gate.shape[2]
    I = (w12.shape[2] - C) // KC
    IR = I - P
    IS = sgu.shape[2] // 2
    SC = [(0, P), (P, P), (2 * P, IS - 2 * P)]
    NB = E + EXTRA
    RC = 6
    TRASH = P
    AHEAD = 8
    assert NT == 8 and KC == 2 and B == 2 and E % 8 == 0 and 0 < IR <= 64 and len(SC) == 3

    x_rows = nc.dram_tensor("x_rows", [NTOK + TRASH, C], F32).ap()
    acc_rows = [nc.dram_tensor(f"acc_rows{j}", [NTOK + TRASH, C], F32).ap() for j in range(2)]

    with ExitStack() as ctx:
        def sb(name, shape, dt=F32):
            return ctx.enter_context(nc.sbuf_tensor(name, shape, dt))

        def sem(name):
            return ctx.enter_context(nc.semaphore(name))

        bank = [ctx.enter_context(nc.psum_tensor(f"bank{i}", [P, 512], F32)) for i in range(8)]

        ident = sb("ident", [P, P])
        tri = sb("tri", [P, P], BF16)
        ones = sb("ones", [P, P], BF16)
        slot_no = sb("slot_no", [P, SLOTS, NT], BF16)
        trash_no = sb("trash_no", [P, 1])
        zeros = sb("zeros", [P, C])
        pace = sb("pace", [P, 1])
        wact_sb = sb("wact_sb", [P, 2 * KC, 2, P])
        wrec_sb = sb("wrec_sb", [P, 2 * KC, C])
        wval_sb = sb("wval_sb", [P, 2, C])
        gate_sb = sb("gate_sb", [P, KC, E])
        sgu_sb = sb("sgu_sb", [P, KC, 2 * IS])
        sda_sb = sb("sda_sb", [P, 2, C])
        sdb_sb = sb("sdb_sb", [SC[2][1], C])
        x_sb = sb("x_sb", [P, NT, C])
        work = sb("work", [P, NT, C])
        work2 = sb("work2", [P, NT, C])
        xnT = sb("xnT", [P, KC, B, T + 1])
        zbuf = sb("zbuf", [P, 3, B * T])
        Z = zbuf[:, 0:2, :].rearrange("p m (b t) -> p m b t", b=B)
        mag2 = zbuf[:, 2, :].rearrange("p (b t) -> p b t", b=B)
        hidT = zbuf
        inv = sb("inv", [P, B, T])
        peak = sb("peak", [P, B, T])
        r4 = sb("r4", [P, NT, C])
        x2n = r4
        x2nT = sb("x2nT", [P, KC, NTOK])
        stats = sb("stats", [P, NT, 6])
        mv = sb("mv", [P, NT, 2])
        rstd = sb("rstd", [P, NT])
        ve = sb("ve", [P, NT])
        nt0 = sb("nt0", [P, NT])
        nt1 = sb("nt1", [P, NT])
        nti = sb("nti", [P, NT], I32)
        lmax = sb("lmax", [P, NT])
        prob = sb("prob", [P, NT, E + 2])
        left = sb("left", [P, NT, E + 2])
        top8 = sb("top8", [P, NT, 8])
        wsum = sb("wsum", [P, NT])
        wnorm = sb("wnorm", [P, NT])
        cw = sb("cw", [P, NT, E])
        mask = sb("mask", [P, NT, E], BF16)
        rank1 = sb("rank1", [P, NB, NT], BF16)
        table = sb("table", [P, NB, NT, RC], BF16)
        rank_f = sb("rank_f", [P, NT, E])
        full = sb("full", [P, E])
        full_i = sb("full_i", [P, E], I32)
        upto = sb("upto", [P, E])
        before = sb("before", [P, E])
        ext_no = sb("ext_no", [P, EXTRA, E])
        ext_e = sb("ext_e", [P, EXTRA, E])
        ext_a = sb("ext_a", [P, EXTRA, E])
        ext_b = sb("ext_b", [P, EXTRA, E])
        ext_s = sb("ext_s", [P, 2, EXTRA])
        ext_i = sb("ext_i", [P, EXTRA + 1], I32)
        over_cw = left[:, :, 0:E]
        hit = sb("hit", [P, 2, SLOTS, NT], BF16)
        tslice = sb("tslice", [P, 2, NT, RC], BF16)
        slot_sum = sb("slot_sum", [P, 2, 4, 2])
        gat_idx = sb("gat_idx", [P, 2, 4], U32)
        sca_idx = sb("sca_idx", [P, 2, 4], U32)
        sca_w = sb("sca_w", [P, 2, 4])
        w12_sb = sb("w12_sb", [P, 8, w12.shape[2]])
        w2b_sb = sb("w2b_sb", [IR, 8, C])
        xg = sb("xg", [P, 8, C])
        xT = sb("xT", [P, 2, KC, P])
        hS = sb("hS", [P, 2, I])
        hT = sb("hT", [P, 2, 2, P])
        yS = sb("yS", [P, 4, C])
        gsil = work2[:, 0:4, :].rearrange("p (a c) d -> p a (c d)", a=2)
        shared = work2[:, :, :]
        y_sh = sb("y_sh", [P, NT, C])
        ow12, ow2b = w12_sb[:, 0, :], w2b_sb[:, 0, :]

        tab_b, x_b, h_b, hT_b, y_b = bank[5], bank[4], (bank[1], bank[6]), (bank[0], bank[7]), bank[2:4]

        x_in = [sem(f"x_in{b}") for b in range(B)]
        w_in = {n: sem(f"in_{n}") for n in ("wact", "wrec", "wval", "gate", "sgu", "sda", "sdb")}
        consts = sem("consts")
        d = sem("d")
        xn_done = sem("xn_done")
        xnT_ps = sem("xnT_ps")
        xnT_act = sem("xnT_act")
        xnT_dve = sem("xnT_dve")
        z_ps = sem("z_ps")
        z_act = sem("z_act")
        z_one = sem("z_one")
        z_sq = sem("z_sq")
        pk = sem("pk")
        inv_act = sem("inv_act")
        kv_done = sem("kv_done")
        r_ps = sem("r_ps")
        r_th = sem("r_th")
        r_one = sem("r_one")
        r_sq = sem("r_sq")
        r4_done = sem("r4_done")
        v_ps = sem("v_ps")
        y_mul = sem("y_mul")
        x2T_ps = sem("x2T_ps")
        x2T_act = sem("x2T_act")
        x2T_dve = sem("x2T_dve")
        lg_ps = sem("lg_ps")
        lg_sub = sem("lg_sub")
        lg_exp = sem("lg_exp")
        mask_done = sem("mask_done")
        rank_ps = sem("rank_ps")
        w_hi = sem("w_hi")
        ext_done = sem("ext_done")
        gu_ps = sem("gu_ps")
        gu_sil = sem("gu_sil")
        gu_mul = sem("gu_mul")
        dn_ps = sem("dn_ps")
        dn_cp = sem("dn_cp")
        xrow_out = sem("xrow_out")
        acc_init = [sem("acc_init0"), sem("acc_init1")]
        hit_done = sem("hit_done")
        tab_ps = sem("tab_ps")
        sum_done = sem("sum_done")
        idx_done = sem("idx_done")
        kept = sem("kept")
        paced = sem("paced")
        gath = [sem(f"gath{j}") for j in range(8)]
        wld = [sem(f"wld{j}") for j in range(4)]
        wld_ext = [sem(f"wld_ext{j}") for j in range(EXTRA)]
        tx_ps = sem("tx_ps")
        xT_done = sem("xT_done")
        h_ps = sem("h_ps")
        h_done = sem("h_done")
        hT_ps = sem("hT_ps")
        hT_done = sem("hT_done")
        y_ps = sem("y_ps")
        y_done = sem("y_done")
        scat = [sem("scat0"), sem("scat1")]
        fin_in = [sem(f"fin_in{j}") for j in range(2)]
        fin_done = sem("fin_done")
        out_done = sem("out_done")
        o_ld = sem("o_ld")
        o_cw = sem("o_cw")
        o_x = sem("o_x")
        o_h_ps = sem("o_h_ps")
        o_h = sem("o_h")
        o_t_ps = sem("o_t_ps")
        o_t = sem("o_t")
        o_y_ps = sem("o_y_ps")
        o_y = sem("o_y")

        HEAD = 10
        LOOPS = (NB - 8 - HEAD) // 8
        TAIL = HEAD + 8 * LOOPS
        LAST = NB + 1

        def pipeline(engine, step):
            for s in range(-1, HEAD):
                step(0, s)
            with engine.Fori(0, LOOPS) as i:
                for u in range(8):
                    step(i, HEAD + u)
            for s in range(TAIL, LAST + 1):
                step(LOOPS, s - 8 * LOOPS)

        def exists(i, c):
            return not isinstance(i, int) or 0 <= 8 * i + c < NB

        def later(i, c, n):
            return not isinstance(i, int) or 8 * i + c >= n

        block = ctx.enter_context(nc.Block())

        @block.sync
        def _(sp):
            xt = x.rearrange("(c p) d -> p c d", p=P)
            for b in range(B):
                sp.dma_start(x_sb[:, TB * b:TB * b + TB, :], xt[:, TB * b:TB * b + TB, :]).then_inc(x_in[b], 16)
            sp.dma_start(wact_sb[:], w_act).then_inc(w_in["wact"], 16)
            sp.dma_start(wrec_sb[:], w_rec).then_inc(w_in["wrec"], 16)
            sp.dma_start(wval_sb[:], w_val).then_inc(w_in["wval"], 16)
            sp.dma_start(gate_sb[:], gate).then_inc(w_in["gate"], 16)
            sp.dma_start(sgu_sb[:], sgu).then_inc(w_in["sgu"], 16)
            sp.dma_start(sda_sb[:], sd_a).then_inc(w_in["sda"], 16)
            sp.dma_start(sdb_sb[:], sd_b).then_inc(w_in["sdb"], 16)

            def load_pair(e, j):
                sp.dma_start(w12_sb[:, 2 * j:2 * j + 2, :],
                             w12[bass.ds(e, 2)].rearrange("e p n -> p e n")).then_inc(wld[j], 16)
                sp.dma_start(w2b_sb[:, 2 * j:2 * j + 2, :],
                             w2b[bass.ds(e, 2)].rearrange("e p n -> p e n")).then_inc(wld[j], 16)

            for j in range(4):
                load_pair(2 * j, j)
            sp.wait_ge(consts, 8)
            sp.dma_start(x_rows[NTOK:NTOK + TRASH, :], zeros[:]).then_inc(xrow_out, 16)
            for j in range(2):
                sp.dma_start(acc_rows[j][NTOK:NTOK + TRASH, :], zeros[:]).then_inc(acc_init[j], 16)
            for c in range(NT):
                sp.dma_start(acc_rows[1][P * c:P * c + P, :], zeros[:]).then_inc(acc_init[1], 16)
            xr = x_rows[0:NTOK, :].rearrange("(c p) d -> p c d", p=P)
            for b in range(B):
                sp.wait_ge(xn_done, NT + TB * (b + 1))
                sp.dma_start(xr[:, TB * b:TB * b + TB, :], x2n[:, TB * b:TB * b + TB, :]).then_inc(xrow_out, 16)
            sp.wait_ge(dn_cp, 4)
            sp.dma_start(acc_rows[0][0:NTOK, :].rearrange("(c p) d -> p c d", p=P), y_sh[:]).then_inc(acc_init[0], 16)
            with sp.Fori(0, E // 8 - 1) as i:
                for j in range(4):
                    sp.wait_ge(y_ps, 8 * i + 2 * j + 2)
                    load_pair(8 * i + 8 + 2 * j, j)
            sp.wait_ge(ext_done, 1)
            for n in range(EXTRA):
                e = sp.value_load(ext_i[0:1, n:n + 1], min_val=0, max_val=E - 1)
                sp.wait_ge(y_ps, E - 8 + n + 1)
                sp.dma_start(w12_sb[:, n, :], w12[bass.ds(e, 1)].rearrange("e p n -> p (e n)")).then_inc(wld_ext[n], 16)
                sp.dma_start(w2b_sb[:, n, :], w2b[bass.ds(e, 1)].rearrange("e p n -> p (e n)")).then_inc(wld_ext[n], 16)
            for j in range(2):
                sp.wait_ge(scat[j], 16 * (NB // 2))
            for h in range(2):
                for j, dst in enumerate((work, work2)):
                    sp.dma_start(dst[:, TB * h:TB * h + TB, :],
                                 acc_rows[j][0:NTOK, :].rearrange("(c p) d -> p c d", p=P)[:, TB * h:TB * h + TB, :]
                                 ).then_inc(fin_in[h], 16)
            with sp.If(sp.value_load(ext_i[0:1, EXTRA:EXTRA + 1], min_val=0, max_val=1)):
                with sp.Fori(0, E) as e:
                    sp.wait_ge(o_y, e * NT + 1)
                    sp.dma_start(ow12, w12[bass.ds(e, 1)].rearrange("e p n -> p (e n)")).then_inc(o_ld, 16)
                    sp.dma_start(ow2b, w2b[bass.ds(e, 1)].rearrange("e p n -> p (e n)")).then_inc(o_ld, 16)
            outv = out.rearrange("(c p) d -> p c d", p=P)
            for h in range(2):
                sp.wait_ge(fin_done, h + 1)
                sp.dma_start(outv[:, TB * h:TB * h + TB, :], work[:, TB * h:TB * h + TB, :]).then_inc(out_done, 16)
            sp.wait_ge(out_done, 32)

        @block.gpsimd
        def _(pool):
            pool.memset(ident[:], 0.0).then_inc(consts, 1)
            pool.wait_ge(consts, 1)
            pool.affine_select(out=ident[:], in_=ident[:], compare_op=ALU.not_equal, fill=1.0, base=0,
                               pattern=[[-1, P]], channel_multiplier=1).then_inc(consts, 1)
            pool.memset(zeros[:], 0.0).then_inc(consts, 1)
            pool.memset(ones[:], 1.0).then_inc(consts, 1)
            pool.wait_ge(consts, 4)
            pool.affine_select(out=tri[:], in_=ones[:], compare_op=ALU.is_gt, fill=0.0, base=0,
                               pattern=[[1, P]], channel_multiplier=-1).then_inc(consts, 1)
            pool.memset(xnT[:, :, :, 0:1], 0.0).then_inc(consts, 1)
            pool.iota(slot_no[:], [[1, SLOTS], [0, NT]], base=1, channel_multiplier=0,
                      allow_small_or_imprecise_dtypes=True).then_inc(consts, 1)
            pool.iota(trash_no[:], [[0, 1]], base=NTOK, channel_multiplier=1,
                      allow_small_or_imprecise_dtypes=True).then_inc(consts, 1)
            pool.iota(table[:, 0:E, :, 0], [[0, E], [P, NT]], base=-NTOK, channel_multiplier=0,
                      allow_small_or_imprecise_dtypes=True).then_inc(consts, 1)
            pool.iota(table[:, 0:E, :, 1], [[0, E], [0, NT]], base=0, channel_multiplier=1,
                      allow_small_or_imprecise_dtypes=True).then_inc(consts, 1)
            pool.memset(prob[:, :, E:E + 2], 2.0).then_inc(consts, 1)
            pool.iota(ext_no[:], [[1, EXTRA], [0, E]], base=0, channel_multiplier=0,
                      allow_small_or_imprecise_dtypes=True).then_inc(consts, 1)
            pool.iota(ext_e[:], [[0, EXTRA], [1, E]], base=0, channel_multiplier=0,
                      allow_small_or_imprecise_dtypes=True).then_inc(consts, 1)
            for k in range(4):
                pool.wait_ge(r_th, k + 1)
                pool.tensor_scalar(r4[:, 2 * k:2 * k + 2, :], r4[:, 2 * k:2 * k + 2, :], 0.0, 1.0,
                                   ALU.max, ALU.add).then_inc(r_one, 1)
            pool.wait_ge(xrow_out, 48)
            pool.wait_ge(acc_init[1], 16 * (NT + 1))


            def await_gather(i, c):
                e = 8 * i + c
                pool.wait_ge(idx_done, 2 * i + c // 4 + 1)
                if later(i, c, 8):
                    pool.wait_ge(tx_ps, e - 7)

            def gather(c):
                pool.indirect_dma_start(xg[:, c % 8, :], None, x_rows, bass.IndirectOffsetOnAxis(
                    ap=gat_idx[:, (c // 4) % 2, c % 4:c % 4 + 1], axis=0)).then_inc(gath[c % 8], 16)

            def await_scatter(i, c):
                e = 8 * i + c
                if later(i, c, 2):
                    pool.wait_ge(scat[c % 2], 64 * i + 16 * (c // 2))
                pool.wait_ge(y_done, e + 1)

            def scatter(c):
                pool.indirect_dma_start(acc_rows[c % 2], bass.IndirectOffsetOnAxis(
                    ap=sca_idx[:, (c // 4) % 2, c % 4:c % 4 + 1], axis=0), yS[:, c % 4, :], None,
                    compute_op=ALU.add).then_inc(scat[c % 2], 16)

            pool.memset(pace[:], 0.0).then_inc(paced, 1)
            for e in range(3):
                await_gather(0, e)
                gather(e)
            pool.wait_ge(acc_init[0], 32)

            def step(i, c):
                if exists(i, c + 4):
                    await_gather(i, c + 4)
                if exists(i, c - 2):
                    await_scatter(i, c - 2)
                if not isinstance(i, int):
                    pool.wait_ge(paced, 8 * i + c - HEAD + 1)
                    pool.tensor_tensor(pace[:, 0:1], trash_no[:], trash_no[:], ALU.add).then_inc(paced, 1)
                if exists(i, c + 4):
                    gather(c + 4)
                if exists(i, c - 2):
                    scatter(c - 2)

            pipeline(pool, step)

        @block.scalar
        def _(act):
            for b in range(B):
                act.wait_ge(xnT_ps, 2 * b + 2)
                act.activation(xnT[:, 1, b, 1:T + 1], bank[2 * b + 1][:], ACT.Copy).then_inc(xnT_act, 1)
            sq = work2[:].rearrange("p c d -> p (c d)").rearrange("p (m b t) -> p m b t", m=2, b=B)
            for b in range(B):
                for m in range(2):
                    act.wait_ge(z_ps, 2 * b + m + 1)
                    act.activation(Z[:, m, b, :], bank[4 + 2 * b + m][:], ACT.Tanh, scale=0.5).then_inc(z_act, 1)
            for b in range(B):
                act.wait_ge(z_one, b + 1)
                act.activation(sq[:, :, b, :], Z[:, :, b, :], ACT.Square).then_inc(z_sq, 1)
            for b in range(B):
                act.wait_ge(pk, b + 1)
                act.activation(inv[:, b, :], peak[:, b, :], ACT.Abs_reciprocal_sqrt).then_inc(inv_act, 1)
            for k in range(4):
                act.wait_ge(r_ps, k + 1)
                act.activation(r4[:, 2 * k:2 * k + 2, :], bank[k][:].rearrange("p (c d) -> p c d", c=2), ACT.Tanh,
                               scale=0.5).then_inc(r_th, 1)
            for k in range(4):
                rk = r4[:, 2 * k:2 * k + 2, :]
                act.wait_ge(r_one, k + 1)
                act.activation(rk, rk, ACT.Square, scale=0.5).then_inc(r_sq, 1)
                act.wait_ge(r_sq, k + 1)
                act.activation(rk, rk, ACT.Square).then_inc(r4_done, 1)
            for b in range(B):
                act.wait_ge(x2T_ps, 2 * b + 2)
                act.activation(x2nT[:, 1, T * b:T * b + T], bank[2 * b + 1][:], ACT.Copy).then_inc(x2T_act, 1)
            act.wait_ge(lg_sub, 1)
            act.activation(prob[:, :, 0:E], prob[:, :, 0:E], ACT.Exp).then_inc(lg_exp, 1)
            for n in range(6):
                rows = SC[n % 3][1]
                act.wait_ge(gu_ps, n + 1)
                if n >= 2:
                    act.wait_ge(gu_mul, n - 1)
                act.activation(gsil[0:rows, n % 2, :], bank[2 * (n % 2)][0:rows, :], ACT.Silu).then_inc(gu_sil, 1)
            for k in range(4):
                act.wait_ge(dn_ps, k + 1)
                act.activation(y_sh[:, 2 * k:2 * k + 2, :], bank[6 + k % 2][:].rearrange("p (c d) -> p c d", c=2),
                               ACT.Copy).then_inc(dn_cp, 1)
            act.wait_ge(ext_done, 1)
            left_over = act.value_load(ext_i[0:1, EXTRA:EXTRA + 1], min_val=0, max_val=1)

            def step(i, c):
                s = 8 * i + c
                if exists(i, c + 1):
                    act.wait_ge(tx_ps, s + 2)
                    if later(i, c, 1):
                        act.wait_ge(h_ps, s)
                    act.activation(xT[:, (c + 1) % 2, :, :], x_b[:, 0:C].rearrange(
                        "p (k t) -> p k t", k=KC), ACT.Copy).then_inc(xT_done, 1)
                if exists(i, c):
                    act.wait_ge(h_ps, s + 1)
                    if later(i, c, 2):
                        act.wait_ge(hT_ps, s - 1)
                    act.activation(hS[:, c % 2, :], h_b[c % 2][:, 0:I], ACT.Silu).then_inc(h_done, 1)
                if exists(i, c - 2):
                    e = s - 2
                    act.wait_ge(y_ps, e + 1)
                    if later(i, c, 6):
                        act.wait_ge(scat[c % 2], 64 * i + 16 * ((c - 6) // 2 + 1))
                    act.wait_ge(kept, 4 * i + 2 * ((c - 2) // 4) + 2)
                    act.activation(yS[:, (c - 2) % 4, :], y_b[c % 2][:, 0:C], ACT.Copy,
                                   scale=sca_w[:, ((c - 2) // 4) % 2, (c - 2) % 4:(c - 2) % 4 + 1]).then_inc(y_done, 1)

            pipeline(act, step)
            with act.If(left_over):
                with act.Fori(0, E * NT) as n:
                    act.wait_ge(o_h_ps, n + 1)
                    act.activation(hS[:, 0, :], h_b[0][:, 0:I], ACT.Silu).then_inc(o_h, 1)

        @block.tensor
        def _(pe):
            pe.wait_ge(consts, 6)
            for b in range(B):
                pe.wait_ge(xn_done, TB * (b + 1))
                for k in range(KC):
                    for j in range(TB):
                        mm = pe.transpose(bank[2 * b + k][:, P * j:P * j + P],
                                          work[:, TB * b + j, P * k:P * k + P], ident[:])
                    mm.then_inc(xnT_ps, 1)
            pe.wait_ge(w_in["wact"], 16)
            for b in range(B):
                pe.wait_ge(xnT_dve, b + 1)
                pe.wait_ge(xnT_act, b + 1)
                for m in range(2):
                    for k in range(2 * KC):
                        late = k // KC
                        mm = pe.matmul(bank[4 + 2 * b + m][:], wact_sb[:, k, m, :], xnT[:, k % KC, b, late:late + T],
                                       start=(k == 0), stop=(k == 2 * KC - 1))
                    mm.then_inc(z_ps, 1)
            pe.wait_ge(w_in["wrec"], 16)
            for c in range(NT):
                b, j = c // TB, c % TB
                for k in range(2 * KC):
                    at = P * j + k // KC
                    mm = pe.matmul(bank[c // 2][:, C * (c % 2):C * (c % 2) + C], xnT[:, k % KC, b, at:at + P],
                                   wrec_sb[:, k, :], start=(k == 0), stop=(k == 2 * KC - 1))
                if c % 2:
                    mm.then_inc(r_ps, 1)
            pe.wait_ge(w_in["wval"], 16)
            pe.wait_ge(kv_done, 1)
            pe.wait_ge(z_act, 4)
            for c in range(NT):
                b, j = c // TB, c % TB
                for m in range(2):
                    mm = pe.matmul(bank[4 + c // 2][:, C * (c % 2):C * (c % 2) + C], Z[:, m, b, P * j:P * j + P],
                                   wval_sb[:, m, :], start=(m == 0), stop=(m == 1))
                if c % 2:
                    mm.then_inc(v_ps, 1)
            pe.wait_ge(r_th, 4)
            for b in range(B):
                pe.wait_ge(xn_done, NT + TB * (b + 1))
                for k in range(KC):
                    for j in range(TB):
                        mm = pe.transpose(bank[2 * b + k][:, P * j:P * j + P],
                                          x2n[:, TB * b + j, P * k:P * k + P], ident[:])
                    mm.then_inc(x2T_ps, 1)
            pe.wait_ge(w_in["gate"], 16)
            pe.wait_ge(x2T_dve, 2)
            pe.wait_ge(x2T_act, 2)
            pe.wait_ge(y_mul, 4)
            for c in range(NT):
                for k in range(KC):
                    mm = pe.matmul(bank[4][:, E * c:E * c + E], x2nT[:, k, P * c:P * c + P], gate_sb[:, k, :],
                                   start=(k == 0), stop=(k == KC - 1))
            mm.then_inc(lg_ps, 1)

            def gate_up(n):
                half, (at, rows) = n // 3, SC[n % 3]
                if n == 0:
                    pe.wait_ge(w_in["sgu"], 16)
                if n >= 2:
                    pe.wait_ge(gu_mul, n - 1)
                for g in range(2):
                    for k in range(KC):
                        mm = pe.matmul(bank[2 * (n % 2) + g][0:rows, :], sgu_sb[:, k, IS * g + at:IS * g + at + rows],
                                       x2nT[:, k, T * half:T * half + T], start=(k == 0), stop=(k == KC - 1))
                mm.then_inc(gu_ps, 1)

            def tables(i, c):
                e = 8 * i + c
                pe.wait_ge(hit_done, 2 * e + 2)
                if c % 4 == 0 and later(i, c, 4):
                    pe.wait_ge(sum_done, 2 * i + c // 4)
                at = RC * (c % 4)
                for t in range(NT):
                    mm = pe.matmul(tab_b[:, at:at + RC], hit[:, c % 2, :, t], tslice[:, c % 2, t, :],
                                   start=(t == 0), stop=(t == NT - 1))
                mm.then_inc(tab_ps, 1)

            gate_up(0)
            pe.wait_ge(mask_done, 1)
            pe.matmul(bank[6][:], tri[:], mask[:].rearrange("p c e -> p (c e)"), start=True, stop=False)
            for t in range(1, NT):
                mm = pe.matmul(bank[6][:, E * t:], ones[:], mask[:, 0:NT - t, :].rearrange("p c e -> p (c e)"),
                               start=False, stop=(t == NT - 1))
            mm.then_inc(rank_ps, 1)
            for t in range(NT):
                mm = pe.matmul(bank[7][:, 0:E], ones[:], mask[:, t, :], start=(t == 0), stop=(t == NT - 1))
            mm.then_inc(rank_ps, 1)
            gate_up(1)
            for e in range(4):
                tables(0, e)
            gate_up(2)
            for e in range(4, 7):
                tables(0, e)
            for n in range(3, 6):
                gate_up(n)
            pe.wait_ge(w_in["sda"], 16)
            pe.wait_ge(w_in["sdb"], 16)
            pe.wait_ge(gu_mul, 6)
            pe.wait_ge(ext_done, 1)
            for c in range(NT):
                if c % 2 == 0 and c >= 4:
                    pe.wait_ge(dn_cp, c // 2 - 1)
                for j, (_, rows) in enumerate(SC):
                    w = sda_sb[:, j, :] if j < 2 else sdb_sb[:]
                    mm = pe.matmul(bank[6 + (c // 2) % 2][:, C * (c % 2):C * (c % 2) + C],
                                   hidT[0:rows, j, P * c:P * c + P], w, start=(j == 0), stop=(j == 2))
                if c % 2:
                    mm.then_inc(dn_ps, 1)
            pe.wait_ge(dn_cp, 4)

            def hidden(dst, xTe, w):
                for k in range(KC):
                    mm = pe.matmul(dst, xTe[:, k, :], w[:, I * k:I * k + I], start=(k == 0), stop=(k == KC - 1))
                return mm

            def turn_hidden(dst, h):
                pe.transpose(dst[:, 0:P], h[:, 0:P], ident[:])
                return pe.transpose(dst[0:IR, P:2 * P], h[:, P:I], ident[:])

            def output(dst, hTe, w, wr):
                pe.matmul(dst, hTe[:, 0, :], w[:, KC * I:KC * I + C], start=True, stop=False)
                return pe.matmul(dst, hTe[0:IR, 1, :], wr, start=False, stop=True)

            left_over = pe.value_load(ext_i[0:1, EXTRA:EXTRA + 1], min_val=0, max_val=1)

            def step(i, c):
                s = 8 * i + c
                if exists(i, c + 1):
                    e, u = s + 1, c + 1
                    pe.wait_ge(gath[u % 8], 16 * i + 16 * (u // 8 + 1))
                    if later(i, c, 0):
                        pe.wait_ge(xT_done, s + 1)
                    for k in range(KC):
                        mm = pe.transpose(x_b[:, P * k:P * k + P],
                                          xg[:, u % 8, P * k:P * k + P], ident[:])
                    mm.then_inc(tx_ps, 1)
                if exists(i, c):
                    if isinstance(i, int) and s >= E:
                        pe.wait_ge(wld_ext[s - E], 32)
                    else:
                        pe.wait_ge(wld[(c // 2) % 4], 32 * i + 32 * (c // 8 + 1))
                    pe.wait_ge(xT_done, s + 1)
                    if later(i, c, 2):
                        pe.wait_ge(h_done, s - 1)
                    hidden(h_b[c % 2][:, 0:I], xT[:, c % 2], w12_sb[:, c % 8]).then_inc(h_ps, 1)
                if exists(i, c - 1):
                    u = c - 1
                    pe.wait_ge(h_done, s)
                    if later(i, c, 3):
                        pe.wait_ge(hT_done, s - 2)
                    turn_hidden(hT_b[u % 2][:, 0:2 * P], hS[:, u % 2]).then_inc(hT_ps, 1)
                if exists(i, c - 2):
                    u = c - 2
                    pe.wait_ge(hT_done, s - 1)
                    if later(i, c, 4):
                        pe.wait_ge(y_done, s - 3)
                    output(y_b[u % 2][:, 0:C], hT[:, u % 2], w12_sb[:, u % 8], w2b_sb[:, u % 8, :]).then_inc(y_ps, 1)
                if exists(i, c + 8):
                    tables(i, c + 8)

            pipeline(pe, step)
            with pe.If(left_over):
                with pe.Fori(0, E * NT) as n:
                    pe.wait_ge(o_x, n + 1)
                    hidden(h_b[0][:, 0:I], xT[:, 0], ow12).then_inc(o_h_ps, 1)
                    pe.wait_ge(o_h, n + 1)
                    turn_hidden(hT_b[0][:, 0:2 * P], hS[:, 0]).then_inc(o_t_ps, 1)
                    pe.wait_ge(o_t, n + 1)
                    output(y_b[0][:, 0:C], hT[:, 0], ow12, ow2b).then_inc(o_y_ps, 1)

        @block.vector
        def _(dve):
            count = [0]

            def mark(ins):
                count[0] += 1
                ins.then_inc(d, 1)

            def settle():
                dve.wait_ge(d, count[0])

            def link(ins):
                mark(ins)
                settle()

            def layer_stats(src, c0):
                cs = slice(c0, c0 + TB)
                for c in range(c0, c0 + TB):
                    mark(dve.bn_stats(stats[:, c, :], src[:, c, :]))
                settle()
                for c in range(c0, c0 + TB):
                    mark(dve.bn_aggr(mv[:, c, :], stats[:, c, :]))
                settle()
                v, y, t0, t1, ti = ve[:, cs], rstd[:, cs], nt0[:, cs], nt1[:, cs], nti[:, cs]
                link(dve.tensor_scalar(v, mv[:, cs, 1], EPS, None, ALU.add))
                link(dve.tensor_scalar(ti, v.bitcast(I32), 1, None, ALU.arith_shift_right))
                link(dve.tensor_scalar(y.bitcast(I32), ti, -1.0, RSQRT_MAGIC, ALU.mult, ALU.add))
                for _ in range(3):
                    link(dve.scalar_tensor_tensor(t0, y, -0.5, y, ALU.mult, ALU.mult))
                    link(dve.tensor_tensor(t1, t0, v, ALU.mult))
                    link(dve.scalar_tensor_tensor(y, t1, 1.5, y, ALU.add, ALU.mult))

            def normalise(dst, src, c):
                return dve.tensor_scalar(dst, src, mv[:, c, 0:1], rstd[:, c:c + 1], ALU.subtract, ALU.mult)

            for b in range(B):
                dve.wait_ge(x_in[b], 16)
                layer_stats(x_sb, TB * b)
                for c in range(TB * b, TB * b + TB):
                    normalise(work[:, c, :], x_sb[:, c, :], c).then_inc(xn_done, 1)
            for b in range(B):
                dve.wait_ge(xnT_ps, 2 * b + 1)
                dve.tensor_copy(xnT[:, 0, b, 1:T + 1], bank[2 * b][:]).then_inc(xnT_dve, 1)

            sq = work2[:].rearrange("p c d -> p (c d)").rearrange("p (m b t) -> p m b t", m=2, b=B)
            for b in range(B):
                dve.wait_ge(z_act, 2 * b + 2)
                dve.tensor_scalar(Z[:, :, b, :], Z[:, :, b, :], 0.0, 1.0, ALU.max, ALU.add).then_inc(z_one, 1)
            for b in range(B):
                dve.wait_ge(z_sq, b + 1)
                link(dve.tensor_tensor(mag2[:, b, :], sq[:, 0, b, :], sq[:, 1, b, :], ALU.add))
                dve.tensor_tensor_scan(peak[:, b, :], mag2[:, b, :], mag2[:, b, :], 0.0, ALU.max, ALU.max).then_inc(pk, 1)
            for b in range(B):
                dve.wait_ge(inv_act, b + 1)
                dve.wait_ge(pk, b + 1)
                link(dve.scalar_tensor_tensor(mag2[:, b, :], inv[:, b, :], -0.5, inv[:, b, :], ALU.mult, ALU.mult))
                link(dve.tensor_tensor(mag2[:, b, :], mag2[:, b, :], peak[:, b, :], ALU.mult))
                link(dve.scalar_tensor_tensor(inv[:, b, :], mag2[:, b, :], 1.5, inv[:, b, :], ALU.add, ALU.mult))
                link(dve.tensor_tensor(Z[:, :, b, :], Z[:, :, b, :], inv[:, b:b + 1, :].to_broadcast([P, 2, T]), ALU.mult))

            def level(first, dist):
                n = (T - 1 - first) // (2 * dist) + 1
                hi = Z[:, :, :, first:T:2 * dist]
                lo = Z[:, :, :, first - dist:T - dist:2 * dist]
                pr = work[:].rearrange("p c d -> p (c d)")[:, 0:4 * n].rearrange("p (m b n) -> p m b n", m=2, b=B)
                pi = work2[:].rearrange("p c d -> p (c d)")[:, 0:4 * n].rearrange("p (m b n) -> p m b n", m=2, b=B)
                mark(dve.tensor_tensor(pr, lo[:, 0:1].to_broadcast([P, 2, B, n]), hi, ALU.mult))
                link(dve.tensor_tensor(pi, lo[:, 1:2].to_broadcast([P, 2, B, n]), hi[:, ::-1], ALU.mult))
                mark(dve.tensor_tensor(hi[:, 0], pr[:, 0], pi[:, 0], ALU.subtract))
                link(dve.tensor_tensor(hi[:, 1], pr[:, 1], pi[:, 1], ALU.add))

            dist = 1
            while dist < T:
                level(2 * dist - 1, dist)
                dist *= 2
            dist = T // 4
            while dist >= 1:
                level(3 * dist - 1, dist)
                dist //= 2
            dve.tensor_copy(nt0[:, 0:1], nt0[:, 0:1]).then_inc(kv_done, 1)

            for b in range(B):
                for k in range(2 * b, 2 * b + 2):
                    dve.wait_ge(v_ps, k + 1)
                    dve.wait_ge(r4_done, k + 1)
                    dve.tensor_tensor(work[:, 2 * k:2 * k + 2, :], bank[4 + k][:].rearrange("p (c d) -> p c d", c=2),
                                      r4[:, 2 * k:2 * k + 2, :], ALU.mult).then_inc(y_mul, 1)
                dve.wait_ge(y_mul, 2 * b + 2)
                layer_stats(work, TB * b)
                for c in range(TB * b, TB * b + TB):
                    mark(normalise(work[:, c, :], work[:, c, :], c))
                settle()
                cs = slice(TB * b, TB * b + TB)
                link(dve.tensor_tensor(x_sb[:, cs, :], x_sb[:, cs, :], work[:, cs, :], ALU.add))
                layer_stats(x_sb, TB * b)
                for c in range(TB * b, TB * b + TB):
                    normalise(x2n[:, c, :], x_sb[:, c, :], c).then_inc(xn_done, 1)
            for b in range(B):
                dve.wait_ge(x2T_ps, 2 * b + 1)
                dve.tensor_copy(x2nT[:, 0, T * b:T * b + T], bank[2 * b][:]).then_inc(x2T_dve, 1)

            lg = bank[4][:].rearrange("p (c e) -> p c e", c=NT)
            dve.wait_ge(lg_ps, 1)
            link(dve.tensor_reduce(lmax[:], lg, AX.X, ALU.max))
            dve.wait_ge(consts, 13)
            dve.tensor_tensor(prob[:, :, 0:E], lg, lmax[:].unsqueeze(2).to_broadcast([P, NT, E]),
                              ALU.subtract).then_inc(lg_sub, 1)
            dve.wait_ge(lg_exp, 1)
            for c in range(NT):
                mark(dve.max(top8[:, c, :], prob[:, c, :]))
            settle()
            for c in range(NT):
                mark(dve.match_replace(left[:, c, :], top8[:, c, :], prob[:, c, :], 0.0))
            settle()
            link(dve.tensor_tensor(cw[:], prob[:, :, 0:E], left[:, :, 0:E], ALU.subtract))
            dve.tensor_scalar(mask[:], cw[:], 0.0, None, ALU.is_gt).then_inc(mask_done, 1)
            link(dve.tensor_reduce(wsum[:], cw[:], AX.X, ALU.add))
            link(dve.reciprocal(wnorm[:], wsum[:]))
            link(dve.tensor_tensor(cw[:], cw[:], wnorm[:].unsqueeze(2).to_broadcast([P, NT, E]), ALU.mult))
            tb = table[:, 0:E, :, :].rearrange("p e c n -> p c e n")
            link(dve.tensor_copy(tb[:, :, :, 3], cw[:]))
            link(dve.tensor_tensor(left[:, :, 0:E], cw[:], tb[:, :, :, 3], ALU.subtract))
            link(dve.tensor_copy(tb[:, :, :, 4], left[:, :, 0:E]))
            link(dve.tensor_tensor(tb[:, :, :, 5], left[:, :, 0:E], tb[:, :, :, 4], ALU.subtract))

            def gate_up(n):
                half, rows = n // 3, SC[n % 3][1]
                dve.wait_ge(gu_sil, n + 1)
                dve.tensor_tensor(hidT[0:rows, n % 3, T * half:T * half + T], gsil[0:rows, n % 2, :],
                                  bank[2 * (n % 2) + 1][0:rows, :], ALU.mult).then_inc(gu_mul, 1)

            gate_up(0)
            dve.wait_ge(rank_ps, 1)
            dve.wait_ge(mask_done, 1)
            link(dve.scalar_tensor_tensor(rank1[:, 0:E, :].rearrange("p e c -> p c e"),
                                          bank[6][:].rearrange("p (c e) -> p c e", c=NT), 1.0, mask[:],
                                          ALU.add, ALU.mult))
            link(dve.tensor_scalar(table[:, 0:E, :, 2], rank1[:, 0:E, :], -1.0, 1.0, ALU.mult, ALU.add))

            def hits(i, c):
                e = 8 * i + c
                if later(i, c, 2):
                    dve.wait_ge(tab_ps, e - 1)
                dve.tensor_tensor(hit[:, c % 2], rank1[:, bass.ds(e, 1), :].to_broadcast([P, SLOTS, NT]), slot_no[:],
                                  ALU.is_equal).then_inc(hit_done, 1)
                dve.tensor_copy(tslice[:, c % 2], table[:, bass.ds(e, 1)].rearrange("p e c n -> p (e c) n")
                                ).then_inc(hit_done, 1)

            def sums(i, c):
                e, r = 8 * i + c, (c // 4) % 2
                dve.wait_ge(tab_ps, e + 1)
                if later(i, c, 8):
                    dve.wait_ge(tx_ps, e - 7)
                dve.tensor_reduce(slot_sum[:, r], tab_b[:, 0:4 * RC].rearrange(
                    "p (e q n) -> p e q n", e=4, q=2), AX.X, ALU.add).then_inc(sum_done, 1)
                dve.wait_ge(sum_done, 2 * i + c // 4 + 1)
                dve.tensor_scalar(gat_idx[:, r], slot_sum[:, r, :, 0], trash_no[:, 0:1], None, ALU.add
                                  ).then_inc(idx_done, 1)

            for e in range(4):
                hits(0, e)
            sums(0, 3)
            gate_up(1)
            for e in range(4, 7):
                hits(0, e)
            gate_up(2)
            dve.wait_ge(rank_ps, 2)
            mark(dve.scalar_tensor_tensor(rank_f[:], bank[6][:].rearrange("p (c e) -> p c e", c=NT), 1.0, mask[:],
                                          ALU.add, ALU.mult))
            link(dve.tensor_scalar(full_i[:], bank[7][:, 0:E], float(SLOTS - 1), None, ALU.add))
            link(dve.tensor_scalar(full_i[:], full_i[:], 7, None, ALU.arith_shift_right))
            link(dve.tensor_scalar(full[:], full_i[:], -1.0, 0.0, ALU.add, ALU.max))
            link(dve.tensor_tensor_scan(upto[:], full[:], zeros[:, 0:E], 0.0, ALU.add, ALU.add))
            link(dve.tensor_tensor(before[:], upto[:], full[:], ALU.subtract))
            shape = [P, EXTRA, E]
            before_b, upto_b = before[:].unsqueeze(1).to_broadcast(shape), upto[:].unsqueeze(1).to_broadcast(shape)
            mark(dve.tensor_tensor(ext_a[:], before_b, ext_no[:], ALU.is_le))
            link(dve.tensor_tensor(ext_b[:], upto_b, ext_no[:], ALU.is_gt))
            link(dve.tensor_tensor(ext_a[:], ext_a[:], ext_b[:], ALU.mult))
            link(dve.tensor_tensor(ext_b[:], ext_a[:], ext_e[:], ALU.mult))
            link(dve.tensor_reduce(ext_s[:, 0, :], ext_b[:], AX.X, ALU.add))
            link(dve.scalar_tensor_tensor(ext_b[:], before_b, float(NT), ext_no[:], ALU.add, ALU.subtract))
            link(dve.tensor_tensor(ext_b[:], ext_a[:], ext_b[:], ALU.mult))
            link(dve.tensor_reduce(ext_s[:, 1, :], ext_b[:], AX.X, ALU.add))
            link(dve.tensor_scalar(ext_s[:, 1, :], ext_s[:, 1, :], float(SLOTS), -float(NTOK + SLOTS), ALU.mult, ALU.add))
            mark(dve.tensor_copy(ext_i[:, 0:EXTRA], ext_s[:, 0, :]))
            link(dve.tensor_scalar(ext_i[:, EXTRA:], upto[:, E - 1:E], float(EXTRA), None, ALU.is_gt))
            dve.tensor_copy(nt0[:, 0:1], ext_s[:, 0, 0:1]).then_inc(ext_done, 1)
            for n in range(EXTRA):
                e = dve.value_load(ext_i[0:1, n:n + 1], min_val=0, max_val=E - 1)
                mark(dve.tensor_scalar(rank1[:, E + n:E + n + 1, :], rank_f[:, :, bass.ds(e, 1)].rearrange("p c e -> p e c"),
                                       ext_s[:, 1, n:n + 1], None, ALU.add))
                link(dve.tensor_copy(table[:, E + n:E + n + 1], table[:, bass.ds(e, 1)]))
                link(dve.tensor_scalar(table[:, E + n, :, 2], rank1[:, E + n, :], -1.0, 1.0, ALU.mult, ALU.add))
            left_over = dve.value_load(ext_i[0:1, EXTRA:EXTRA + 1], min_val=0, max_val=1)
            for n in range(3, 6):
                gate_up(n)
            def step(i, c):
                s = 8 * i + c
                if exists(i, c + 8):
                    hits(i, c + 8)
                if c % 4 == 1 and exists(i, c - 1):
                    g, r = 2 * i + (c - 1) // 4, ((c - 1) // 4) % 2
                    if later(i, c, 9):
                        for j in range(2):
                            dve.wait_ge(scat[j], 64 * i + 16 * ((c - 7) // 2 + 1))
                        dve.wait_ge(y_done, s - 5)
                    dve.tensor_copy(sca_idx[:, r], gat_idx[:, r]).then_inc(kept, 1)
                    dve.tensor_copy(sca_w[:, r], slot_sum[:, r, :, 1]).then_inc(kept, 1)
                if exists(i, c - 1):
                    dve.wait_ge(hT_ps, s)
                    if later(i, c, 3):
                        dve.wait_ge(y_ps, s - 2)
                    u = (c - 1) % 2
                    dve.tensor_copy(hT[:, u].rearrange("p k t -> p (k t)"), hT_b[u][:, 0:2 * P]
                                    ).then_inc(hT_done, 1)
                if (c + 7) % 4 == 3 and exists(i, c + 7):
                    sums(i, c + 7)

            pipeline(dve, step)

            with dve.If(left_over):
                for h in range(2):
                    dve.wait_ge(fin_in[h], 32)
                block_i = left[:, :, 0:E].bitcast(I32)
                dve.tensor_scalar(block_i, rank_f[:], float(SLOTS - 1), None, ALU.add).then_inc(o_cw, 1)
                dve.wait_ge(o_cw, 1)
                dve.tensor_scalar(block_i, block_i, 7, None, ALU.arith_shift_right).then_inc(o_cw, 1)
                dve.wait_ge(o_cw, 2)
                dve.tensor_copy(rank_f[:], block_i).then_inc(o_cw, 1)
                dve.wait_ge(o_cw, 3)
                dve.scalar_tensor_tensor(cw[:], rank_f[:], 1.5, cw[:], ALU.is_gt, ALU.mult).then_inc(o_cw, 1)
                dve.wait_ge(o_cw, 4)
                dve.tensor_tensor(rank_f[:], rank_f[:], before[:].unsqueeze(1).to_broadcast([P, NT, E]),
                                  ALU.add).then_inc(o_cw, 1)
                dve.wait_ge(o_cw, 5)
                dve.scalar_tensor_tensor(over_cw, rank_f[:], EXTRA + 1.5, cw[:], ALU.is_gt, ALU.mult).then_inc(o_y, 1)
                with dve.Fori(0, E) as e:
                    dve.wait_ge(o_y, e * NT + 1)
                    dve.wait_ge(o_ld, 32 * e + 32)
                    for c in range(NT):
                        n = e * NT + c
                        dve.tensor_copy(xT[:, 0], x2nT[:, :, P * c:P * c + P]).then_inc(o_x, 1)
                        dve.wait_ge(o_t_ps, n + 1)
                        dve.tensor_copy(hT[:, 0].rearrange("p k t -> p (k t)"), hT_b[0][:, 0:2 * P]).then_inc(o_t, 1)
                        dve.wait_ge(o_y_ps, n + 1)
                        dve.scalar_tensor_tensor(work[:, c, :], y_b[0][:, 0:C], over_cw[:, c, bass.ds(e, 1)],
                                                 work[:, c, :], ALU.mult, ALU.add).then_inc(o_y, 1)
                dve.wait_ge(o_y, E * NT + 1)

            for h in range(2):
                cs = slice(TB * h, TB * h + TB)
                dve.wait_ge(fin_in[h], 32)
                link(dve.tensor_tensor(work[:, cs, :], work[:, cs, :], work2[:, cs, :], ALU.add))
                layer_stats(work, TB * h)
                for c in range(TB * h, TB * h + TB):
                    mark(normalise(work[:, c, :], work[:, c, :], c))
                settle()
                dve.tensor_tensor(work[:, cs, :], work[:, cs, :], x_sb[:, cs, :], ALU.add).then_inc(fin_done, 1)


def kernel(L0_attn_x, L0_attn_W_act, L0_attn_W_val, L0_attn_W_rec, L0_ffn_gate_w, L0_ffn_experts_w1,
           L0_ffn_experts_w2, L0_ffn_shared_gate_up, L0_ffn_shared_down):
    import numpy as np
    import concourse.bacc as bacc
    from concourse.bass_utils import run_bass_kernel_spmd

    x = np.asarray(L0_attn_x)
    bx, tx, C = x.shape
    KC = C // P
    E, I, _ = L0_ffn_experts_w1.shape
    IS = L0_ffn_shared_down.shape[1]

    def by_k(w):
        w = np.asarray(w)
        return w.T.reshape(w.shape[1] // P, P, w.shape[0]).transpose(1, 0, 2)

    w_act = by_k(L0_attn_W_act).reshape(P, 2 * KC, C // 2, 2).transpose(0, 1, 3, 2)
    w_val = np.asarray(L0_attn_W_val).T.reshape(C // 2, 2, C)
    w1 = np.asarray(L0_ffn_experts_w1).transpose(0, 2, 1).reshape(E, KC, P, I).transpose(0, 2, 1, 3).reshape(E, P, KC * I)
    w2 = np.asarray(L0_ffn_experts_w2).transpose(0, 2, 1)
    sd = np.asarray(L0_ffn_shared_down).T
    arrays = {
        "x": x.reshape(bx * tx, C),
        "w_act": w_act,
        "w_rec": by_k(L0_attn_W_rec),
        "w_val": w_val,
        "gate": by_k(L0_ffn_gate_w),
        "w12": np.concatenate([w1, w2[:, 0:P, :]], axis=2),
        "w2b": w2[:, P:, :],
        "sgu": by_k(L0_ffn_shared_gate_up),
        "sd_a": sd[0:2 * P].reshape(2, P, C).transpose(1, 0, 2),
        "sd_b": sd[2 * P:],
    }
    arrays = {n: np.ascontiguousarray(a) for n, a in arrays.items()}
    nc = bacc.Bacc("TRN2", target_bir_lowering=False, num_devices=1)
    aps = {n: nc.dram_tensor(n, a.shape, F32, kind="ExternalInput").ap() for n, a in arrays.items()}
    out = nc.dram_tensor("out", (bx * tx, C), F32, kind="ExternalOutput").ap()
    moe_block(nc, out=out, **aps)
    r = run_bass_kernel_spmd(nc, [arrays], core_ids=[0])
    return r.results[0]["out"].reshape(bx, tx, C)
```

```python
from contextlib import ExitStack

import concourse.bass as bass
from concourse import mybir

F32 = mybir.dt.float32
BF16 = mybir.dt.bfloat16
I32 = mybir.dt.int32
U32 = mybir.dt.uint32
ALU = mybir.AluOpType
ACT = mybir.ActivationFunctionType
AX = mybir.AxisListType

P = 128
EPS = 1e-5
TOPK = 6
SLOTS = P
EXTRA = 2
ACCS = 4


def moe_block(nc, x, w_act, w_rec, w_val, gate, w12, w2b, sgu, sd_a, sd_b, out):
    NTOK, C = x.shape
    NT = NTOK // P
    B = 2
    T = NTOK // B
    TB = T // P
    KC = C // P
    E = gate.shape[2]
    I = (w12.shape[2] - C) // KC
    IR = I - P
    IS = sgu.shape[2] // 2
    SC = [(0, P), (P, P), (2 * P, IS - 2 * P)]
    NB = E + EXTRA
    RC = 6
    TRASH = P
    AHEAD = 8
    assert NT == 8 and KC == 2 and B == 2 and E % 8 == 0 and 0 < IR <= 64 and len(SC) == 3

    x_rows = nc.dram_tensor("x_rows", [NTOK + TRASH, C], F32).ap()
    acc_rows = [nc.dram_tensor(f"acc_rows{j}", [NTOK + TRASH, C], F32).ap() for j in range(ACCS)]

    with ExitStack() as ctx:
        def sb(name, shape, dt=F32):
            return ctx.enter_context(nc.sbuf_tensor(name, shape, dt))

        def sem(name):
            return ctx.enter_context(nc.semaphore(name))

        bank = [ctx.enter_context(nc.psum_tensor(f"bank{i}", [P, 512], F32)) for i in range(8)]

        ident = sb("ident", [P, P])
        tri = sb("tri", [P, P], BF16)
        ones = sb("ones", [P, P], BF16)
        slot_no = sb("slot_no", [P, SLOTS, NT], BF16)
        trash_no = sb("trash_no", [P, 1])
        zeros = sb("zeros", [P, C])
        half_one = sb("half_one", [P, 2])
        pace = sb("pace", [P, 1])
        wact_sb = sb("wact_sb", [P, 2 * KC, 2, P])
        wrec_sb = sb("wrec_sb", [P, 2 * KC, C])
        wval_sb = sb("wval_sb", [P, 2, C])
        gate_sb = sb("gate_sb", [P, KC, E])
        sgu_sb = sb("sgu_sb", [P, KC, 2 * IS])
        sda_sb = sb("sda_sb", [P, 2, C])
        sdb_sb = sb("sdb_sb", [SC[2][1], C])
        x_sb = sb("x_sb", [P, NT, C])
        work = sb("work", [P, NT, C])
        work2 = sb("work2", [P, NT, C])
        xnT = sb("xnT", [P, KC, B, T + 1])
        zbuf = sb("zbuf", [P, 2 * B * T])
        Z = zbuf[:].rearrange("p (m b t) -> p m b t", m=2, b=B)
        mag2 = sb("mag2", [P, B, T])
        prod = sb("prod", [P, 2, T])
        hidT = sb("hidT", [P, 3, NTOK])
        inv = sb("inv", [P, B, T])
        peak = sb("peak", [P, B, T])
        r4 = sb("r4", [P, NT, C])
        x2n = r4
        x2nT = sb("x2nT", [P, KC, NTOK])
        stats = sb("stats", [P, NT, 6])
        mv = sb("mv", [P, NT, 2])
        rstd = sb("rstd", [P, NT])
        shift = sb("shift", [P, NT])
        ve = sb("ve", [P, NT])
        rs0 = sb("rs0", [P, NT])
        nt0 = sb("nt0", [P, NT])
        nt1 = sb("nt1", [P, NT])
        lmax = sb("lmax", [P, NT])
        below = sb("below", [P, NT, E + 2])
        prob = sb("prob", [P, NT, E])
        left = sb("left", [P, NT, E + 2])
        top8 = sb("top8", [P, NT, 8])
        wsum = sb("wsum", [P, NT])
        wnorm = sb("wnorm", [P, NT])
        cw = sb("cw", [P, NT, E])
        mask = sb("mask", [P, NT, E], BF16)
        rank1 = sb("rank1", [P, NB + 1, NT], BF16)
        table = sb("table", [P, NB + 1, NT, RC], BF16)
        rank_f = sb("rank_f", [P, NT, E])
        full = sb("full", [P, E])
        full_i = sb("full_i", [P, E], I32)
        upto = sb("upto", [P, E])
        before = sb("before", [P, E])
        ext_no = sb("ext_no", [P, EXTRA, E])
        ext_e = sb("ext_e", [P, EXTRA, E])
        ext_a = sb("ext_a", [P, EXTRA, E])
        ext_b = sb("ext_b", [P, EXTRA, E])
        ext_s = sb("ext_s", [P, 2, EXTRA])
        ext_i = sb("ext_i", [P, EXTRA + 1], I32)
        over_cw = left[:, :, 0:E]
        hit = sb("hit", [P, 2, SLOTS, NT], BF16)
        tslice = sb("tslice", [P, 2, NT, RC], BF16)
        slot_sum = sb("slot_sum", [P, 4, 4, 2])
        gat_idx = sb("gat_idx", [P, 4, 4], U32)
        w12_sb = sb("w12_sb", [P, 8, w12.shape[2]])
        w2b_sb = sb("w2b_sb", [IR, 8, C])
        xg = sb("xg", [P, 8, C])
        xT = sb("xT", [P, 2, KC, P])
        hS = sb("hS", [P, 2, I])
        hT = sb("hT", [P, 2, 2, P])
        yS = sb("yS", [P, 8, C])
        sq = work2[:].rearrange("p (b h) d -> p b (h d)", b=B).rearrange("p b (m t) -> p m b t", m=2)
        gsil = work2[:, 0:4, :].rearrange("p (a c) d -> p a (c d)", a=2)
        part = (work, work2, zbuf[:].rearrange("p (c d) -> p c d", c=NT),
                hidT[:, 0:2, :].rearrange("p k n -> p (k n)").rearrange("p (c d) -> p c d", c=NT))
        y_sh = sb("y_sh", [P, NT, C])
        ow12, ow2b = w12_sb[:, 0, :], w2b_sb[:, 0, :]

        tab_b, x_b, h_b, hT_b, y_b = bank[5], bank[4], (bank[1], bank[6]), (bank[0], bank[7]), bank[2:4]
        x2T_b = ((bank[0], bank[1]), (bank[6], bank[7]))
        dn_b = (bank[5], bank[0], bank[2], bank[3])

        x_in = [sem(f"x_in{k}") for k in range(4)]
        w_in = {n: sem(f"in_{n}") for n in ("wact", "wrec", "wval", "gate", "sgu", "sda", "sdb")}
        consts = sem("consts")
        d = sem("d")
        var_done = sem("var_done")
        rs_act = sem("rs_act")
        rstd_done = sem("rstd_done")
        shift_done = sem("shift_done")
        norm_dve = sem("norm_dve")
        norm_act = sem("norm_act")
        xnT_ps = sem("xnT_ps")
        xnT_act = sem("xnT_act")
        xnT_dve = sem("xnT_dve")
        z_ps = sem("z_ps")
        z_th = sem("z_th")
        z_relu = sem("z_relu")
        z_sq = sem("z_sq")
        mag_done = sem("mag_done")
        pk = sem("pk")
        inv_act = sem("inv_act")
        newton = sem("newton")
        kv_done = sem("kv_done")
        r_ps = sem("r_ps")
        r_th = sem("r_th")
        r_relu = sem("r_relu")
        r_sq = sem("r_sq")
        r4_done = sem("r4_done")
        v_ps = sem("v_ps")
        y_mul = sem("y_mul")
        x2T_ps = sem("x2T_ps")
        x2T_act = sem("x2T_act")
        x2T_dve = sem("x2T_dve")
        lg_ps = sem("lg_ps")
        lg_sub = sem("lg_sub")
        lg_exp = sem("lg_exp")
        mask_done = sem("mask_done")
        rank_ps = sem("rank_ps")
        rank_read = sem("rank_read")
        ext_done = sem("ext_done")
        gu_ps = sem("gu_ps")
        gu_sil = sem("gu_sil")
        gu_mul = sem("gu_mul")
        dn_ps = sem("dn_ps")
        dn_cp = sem("dn_cp")
        xrow_out = sem("xrow_out")
        acc_init = [sem(f"acc_init{j}") for j in range(ACCS)]
        hit_done = sem("hit_done")
        tab_ps = sem("tab_ps")
        sum_done = sem("sum_done")
        idx_done = sem("idx_done")
        paced = sem("paced")
        gath = [sem(f"gath{j}") for j in range(8)]
        wld = [sem(f"wld{j}") for j in range(4)]
        wld_ext = [sem(f"wld_ext{j}") for j in range(EXTRA)]
        tx_ps = sem("tx_ps")
        xT_done = sem("xT_done")
        h_ps = sem("h_ps")
        h_done = sem("h_done")
        hT_ps = sem("hT_ps")
        hT_done = sem("hT_done")
        y_ps = sem("y_ps")
        y_done = sem("y_done")
        scat = [sem(f"scat{j}") for j in range(ACCS)]
        part_in = sem("part_in")
        fin_in1 = [sem(f"fin_in1{q}") for q in range(4)]
        fin_in = [sem(f"fin_in{q}") for q in range(4)]
        sum_pool = sem("sum_pool")
        fin_pool = sem("fin_pool")
        fin_dve = sem("fin_dve")
        out_done = sem("out_done")
        o_ld = sem("o_ld")
        o_cw = sem("o_cw")
        o_x = sem("o_x")
        o_h_ps = sem("o_h_ps")
        o_h = sem("o_h")
        o_t_ps = sem("o_t_ps")
        o_t = sem("o_t")
        o_y_ps = sem("o_y_ps")
        o_y = sem("o_y")

        TURN = 16
        HEAD = 10
        LOOPS = (NB - 8 - HEAD) // TURN
        TAIL = HEAD + TURN * LOOPS
        LAST = NB + 1

        def pipeline(engine, step):
            for s in range(-1, HEAD):
                step(0, s)
            with engine.Fori(0, LOOPS) as i:
                for u in range(TURN):
                    step(i, HEAD + u)
            for s in range(TAIL, LAST + 1):
                step(LOOPS, s - TURN * LOOPS)

        assert ACCS == 4
        acc_by_block = [e % ACCS if e < TAIL - 2 else (0, 1, 3)[(e - TAIL + 2) % 3] for e in range(NB)]
        adds = [acc_by_block.count(j) for j in range(ACCS)]

        def acc_of(i, c):
            return acc_by_block[TURN * i + c] if isinstance(i, int) else c % ACCS

        def added(i, c):
            e = TURN * i + c
            return 16 * acc_by_block[:e].count(acc_by_block[e]) if isinstance(i, int) else 64 * i + 16 * (c // ACCS)

        def exists(i, c):
            return not isinstance(i, int) or 0 <= TURN * i + c < NB

        def has_table(i, c):
            return not isinstance(i, int) or TURN * i + c <= NB

        def later(i, c, n):
            return not isinstance(i, int) or TURN * i + c >= n

        block = ctx.enter_context(nc.Block())

        @block.sync
        def _(sp):
            xt = x.rearrange("(c p) d -> p c d", p=P)
            for k in range(4):
                sp.dma_start(x_sb[:, 2 * k:2 * k + 2, :], xt[:, 2 * k:2 * k + 2, :]).then_inc(x_in[k], 16)
            sp.dma_start(wact_sb[:], w_act).then_inc(w_in["wact"], 16)
            sp.dma_start(wrec_sb[:], w_rec).then_inc(w_in["wrec"], 16)
            sp.dma_start(wval_sb[:], w_val).then_inc(w_in["wval"], 16)
            sp.dma_start(gate_sb[:], gate).then_inc(w_in["gate"], 16)
            sp.dma_start(sgu_sb[:], sgu).then_inc(w_in["sgu"], 16)
            sp.dma_start(sda_sb[:], sd_a).then_inc(w_in["sda"], 16)
            sp.dma_start(sdb_sb[:], sd_b).then_inc(w_in["sdb"], 16)

            def rows_of(j, q):
                return acc_rows[j][2 * P * q:2 * P * q + 2 * P, :].rearrange("(c p) d -> p c d", p=P)

            def load_pair(e, j):
                sp.dma_start(w12_sb[:, 2 * j:2 * j + 2, :],
                             w12[bass.ds(e, 2)].rearrange("e p n -> p e n")).then_inc(wld[j], 16)
                sp.dma_start(w2b_sb[:, 2 * j:2 * j + 2, :],
                             w2b[bass.ds(e, 2)].rearrange("e p n -> p e n")).then_inc(wld[j], 16)

            for j in range(4):
                load_pair(2 * j, j)
            sp.wait_ge(consts, 10)
            sp.dma_start(x_rows[NTOK:NTOK + TRASH, :], zeros[:]).then_inc(xrow_out, 16)
            for j in range(ACCS):
                sp.dma_start(acc_rows[j][NTOK:NTOK + TRASH, :], zeros[:]).then_inc(acc_init[j], 16)
                if j:
                    for c in range(NT):
                        sp.dma_start(acc_rows[j][P * c:P * c + P, :], zeros[:]).then_inc(acc_init[j], 16)
            xr = x_rows[0:NTOK, :].rearrange("(c p) d -> p c d", p=P)
            for b in range(B):
                sp.wait_ge(norm_dve, 8 + 4 * b)
                sp.wait_ge(norm_act, 8 + 4 * b)
                sp.dma_start(xr[:, TB * b:TB * b + TB, :], x2n[:, TB * b:TB * b + TB, :]).then_inc(xrow_out, 16)
            for b in range(B):
                sp.wait_ge(dn_cp, 2 * b + 2)
                sp.dma_start(acc_rows[0][T * b:T * b + T, :].rearrange("(c p) d -> p c d", p=P),
                             y_sh[:, TB * b:TB * b + TB, :]).then_inc(acc_init[0], 16)
            with sp.Fori(0, E // 8 - 1) as i:
                for j in range(4):
                    sp.wait_ge(y_ps, 8 * i + 2 * j + 2)
                    load_pair(8 * i + 8 + 2 * j, j)
            sp.wait_ge(ext_done, 1)
            for n in range(EXTRA):
                e = sp.value_load(ext_i[0:1, n:n + 1], min_val=0, max_val=E - 1)
                sp.wait_ge(y_ps, E - 8 + n + 1)
                sp.dma_start(w12_sb[:, n, :], w12[bass.ds(e, 1)].rearrange("e p n -> p (e n)")).then_inc(wld_ext[n], 16)
                sp.dma_start(w2b_sb[:, n, :], w2b[bass.ds(e, 1)].rearrange("e p n -> p (e n)")).then_inc(wld_ext[n], 16)
            sp.wait_ge(scat[2], 16 * adds[2])
            for q in range(4):
                sp.wait_ge(y_ps, E - 3 + q)
                sp.dma_start(part[2][:, 2 * q:2 * q + 2, :], rows_of(2, q)).then_inc(part_in, 16)
            for j in (1, 3, 0):
                sp.wait_ge(scat[j], 16 * adds[j])
                if j == 1:
                    for q in range(2):
                        sp.dma_start(part[1][:, 2 * q:2 * q + 2, :], rows_of(1, q)).then_inc(fin_in1[q], 16)
            for q in range(4):
                for j in (1, 3, 0) if q >= 2 else (3, 0):
                    sp.dma_start(part[j][:, 2 * q:2 * q + 2, :], rows_of(j, q)).then_inc(
                        fin_in1[q] if j == 1 else fin_in[q], 16)
            with sp.If(sp.value_load(ext_i[0:1, EXTRA:EXTRA + 1], min_val=0, max_val=1)):
                with sp.Fori(0, E) as e:
                    sp.wait_ge(o_y, e * NT + 1)
                    sp.dma_start(ow12, w12[bass.ds(e, 1)].rearrange("e p n -> p (e n)")).then_inc(o_ld, 16)
                    sp.dma_start(ow2b, w2b[bass.ds(e, 1)].rearrange("e p n -> p (e n)")).then_inc(o_ld, 16)
            outv = out.rearrange("(c p) d -> p c d", p=P)
            for k in range(4):
                if k < 2:
                    sp.wait_ge(fin_pool, k + 1)
                else:
                    sp.wait_ge(fin_dve, k - 1)
                sp.dma_start(outv[:, 2 * k:2 * k + 2, :], work[:, 2 * k:2 * k + 2, :]).then_inc(out_done, 16)
            sp.wait_ge(out_done, 64)

        @block.gpsimd
        def _(pool):
            pool.memset(ident[:], 0.0).then_inc(consts, 1)
            pool.wait_ge(consts, 1)
            pool.affine_select(out=ident[:], in_=ident[:], compare_op=ALU.not_equal, fill=1.0, base=0,
                               pattern=[[-1, P]], channel_multiplier=1).then_inc(consts, 1)
            pool.memset(half_one[:, 0:1], 0.5).then_inc(consts, 1)
            pool.memset(half_one[:, 1:2], 1.0).then_inc(consts, 1)
            pool.memset(zeros[:], 0.0).then_inc(consts, 1)
            pool.memset(ones[:], 1.0).then_inc(consts, 1)
            pool.wait_ge(consts, 6)
            pool.affine_select(out=tri[:], in_=ones[:], compare_op=ALU.is_gt, fill=0.0, base=0,
                               pattern=[[1, P]], channel_multiplier=-1).then_inc(consts, 1)
            pool.memset(xnT[:, :, :, 0:1], 0.0).then_inc(consts, 1)
            pool.iota(slot_no[:], [[1, SLOTS], [0, NT]], base=1, channel_multiplier=0,
                      allow_small_or_imprecise_dtypes=True).then_inc(consts, 1)
            pool.iota(trash_no[:], [[0, 1]], base=NTOK, channel_multiplier=1,
                      allow_small_or_imprecise_dtypes=True).then_inc(consts, 1)
            pool.iota(table[:, 0:E, :, 0], [[0, E], [P, NT]], base=-NTOK, channel_multiplier=0,
                      allow_small_or_imprecise_dtypes=True).then_inc(consts, 1)
            pool.iota(table[:, 0:E, :, 1], [[0, E], [0, NT]], base=0, channel_multiplier=1,
                      allow_small_or_imprecise_dtypes=True).then_inc(consts, 1)
            pool.memset(rank1[:, NB:, :], 0.0).then_inc(consts, 1)
            pool.memset(table[:, NB:, :, :], 0.0).then_inc(consts, 1)
            pool.memset(below[:, :, E:E + 2], 2.0).then_inc(consts, 1)
            pool.iota(ext_no[:], [[1, EXTRA], [0, E]], base=0, channel_multiplier=0,
                      allow_small_or_imprecise_dtypes=True).then_inc(consts, 1)
            pool.iota(ext_e[:], [[0, EXTRA], [1, E]], base=0, channel_multiplier=0,
                      allow_small_or_imprecise_dtypes=True).then_inc(consts, 1)
            pool.wait_ge(z_sq, 4)
            pool.tensor_tensor(mag2[:, 1, :], sq[:, 0, 1, :], sq[:, 1, 1, :], ALU.add).then_inc(mag_done, 1)
            pool.wait_ge(inv_act, 2)
            pool.wait_ge(pk, 2)
            pool.tensor_tensor(mag2[:, 1, :], inv[:, 1, :], inv[:, 1, :], ALU.mult).then_inc(newton, 1)
            pool.wait_ge(newton, 1)
            pool.tensor_tensor(mag2[:, 1, :], mag2[:, 1, :], peak[:, 1, :], ALU.mult).then_inc(newton, 1)
            pool.wait_ge(newton, 2)
            pool.tensor_scalar(mag2[:, 1, :], mag2[:, 1, :], -0.5, 1.5, ALU.mult, ALU.add).then_inc(newton, 1)
            pool.wait_ge(newton, 3)
            pool.tensor_tensor(inv[:, 1, :], mag2[:, 1, :], inv[:, 1, :], ALU.mult).then_inc(newton, 1)
            pool.wait_ge(xrow_out, 48)
            for j in range(1, ACCS):
                pool.wait_ge(acc_init[j], 16 * (NT + 1))

            def await_gather(i, c):
                e = TURN * i + c
                pool.wait_ge(idx_done, 4 * i + c // 4 + 1)
                if later(i, c, 8):
                    pool.wait_ge(tx_ps, e - 7)

            def gather(c):
                pool.indirect_dma_start(xg[:, c % 8, :], None, x_rows, bass.IndirectOffsetOnAxis(
                    ap=gat_idx[:, (c // 4) % 4, c % 4:c % 4 + 1], axis=0)).then_inc(gath[c % 8], 16)

            def await_scatter(i, c):
                e = TURN * i + c
                if later(i, c, ACCS):
                    pool.wait_ge(scat[acc_of(i, c)], added(i, c))
                pool.wait_ge(y_done, e + 1)

            def scatter(i, c):
                pool.indirect_dma_start(acc_rows[acc_of(i, c)], bass.IndirectOffsetOnAxis(
                    ap=gat_idx[:, (c // 4) % 4, c % 4:c % 4 + 1], axis=0), yS[:, c % 8, :], None,
                    compute_op=ALU.add).then_inc(scat[acc_of(i, c)], 16)

            pool.memset(pace[:], 0.0).then_inc(paced, 1)
            for e in range(3):
                await_gather(0, e)
                gather(e)

            def step(i, c):
                if isinstance(i, int):
                    if exists(i, c + 4):
                        await_gather(i, c + 4)
                        gather(c + 4)
                    s = TURN * i + c
                    if s == 2:
                        pool.wait_ge(acc_init[0], 48)
                    for u in {HEAD - 2: (), HEAD - 1: (), TAIL: (c - 4, c - 3, c - 2)}.get(s, (c - 2,)):
                        if exists(i, u):
                            await_scatter(i, u)
                            scatter(i, u)
                elif c % 2 == 0:
                    for u in (c, c + 1):
                        await_gather(i, u + 4)
                        await_scatter(i, u - 4)
                    pool.wait_ge(paced, TURN // 2 * i + (c - HEAD) // 2 + 1)
                    pool.tensor_tensor(pace[:, 0:1], trash_no[:], trash_no[:], ALU.add).then_inc(paced, 1)
                    for u in (c, c + 1):
                        gather(u + 4)
                        scatter(i, u - 4)

            pipeline(pool, step)
            pool.wait_ge(part_in, 64)
            for q in range(4):
                cs = slice(2 * q, 2 * q + 2)
                pool.wait_ge(fin_in1[q], 16)
                pool.tensor_tensor(part[2][:, cs, :], part[2][:, cs, :], work2[:, cs, :], ALU.add).then_inc(sum_pool, 1)
            for k in range(2):
                cs = slice(2 * k, 2 * k + 2)
                pool.wait_ge((norm_dve, norm_act)[k], 14)
                pool.tensor_tensor(work[:, cs, :], work[:, cs, :], x_sb[:, cs, :], ALU.add).then_inc(fin_pool, 1)

        @block.scalar
        def _(act):
            def first_rsqrt(q, c0):
                act.wait_ge(var_done, q + 1)
                act.activation(rs0[:, c0:c0 + TB], ve[:, c0:c0 + TB], ACT.Abs_reciprocal_sqrt).then_inc(rs_act, 1)

            def normalise(q, dst, src, c0):
                act.wait_ge(rstd_done, q + 1)
                act.wait_ge(shift_done, q + 1)
                for c in (c0 + 2, c0 + 3):
                    act.activation(dst[:, c, :], src[:, c, :], ACT.Identity, bias=shift[:, c:c + 1],
                                   scale=rstd[:, c:c + 1]).then_inc(norm_act, 1)

            def gate_z(b):
                for m in range(2):
                    n = 2 * b + m
                    act.wait_ge(z_ps, n + 1)
                    act.activation(Z[:, m, b, :], bank[4 + n][:], ACT.Tanh, scale=0.5).then_inc(z_th, 1)
                    act.wait_ge(z_th, n + 1)
                    act.activation(Z[:, m, b, :], Z[:, m, b, :], ACT.Relu).then_inc(z_relu, 1)
                    act.wait_ge(z_relu, n + 1)
                    act.activation(sq[:, m, b, :], Z[:, m, b, :], ACT.Square, bias=half_one[:, 1:2]).then_inc(z_sq, 1)

            def first_inv(b):
                act.wait_ge(pk, b + 1)
                act.activation(inv[:, b, :], peak[:, b, :], ACT.Abs_reciprocal_sqrt).then_inc(inv_act, 1)

            def gate_r(k):
                rk = r4[:, 2 * k:2 * k + 2, :]
                act.wait_ge(r_ps, k + 1)
                act.activation(rk, bank[k][:].rearrange("p (c d) -> p c d", c=2), ACT.Tanh, scale=0.5).then_inc(r_th, 1)
                act.wait_ge(r_th, k + 1)
                act.activation(rk, rk, ACT.Relu).then_inc(r_relu, 1)
                act.wait_ge(r_relu, k + 1)
                act.activation(rk, rk, ACT.Square, scale=0.5, bias=half_one[:, 0:1]).then_inc(r_sq, 1)
                act.wait_ge(r_sq, k + 1)
                act.activation(rk, rk, ACT.Square).then_inc(r4_done, 1)

            def gate_silu(n):
                rows = SC[n % 3][1]
                act.wait_ge(gu_ps, n + 1)
                if n >= 2:
                    act.wait_ge(gu_mul, n - 1)
                act.activation(gsil[0:rows, n % 2, :], bank[2 * (n % 2)][0:rows, :], ACT.Silu).then_inc(gu_sil, 1)

            def copy_down(k):
                act.wait_ge(dn_ps, k + 1)
                act.activation(y_sh[:, 2 * k:2 * k + 2, :], dn_b[k][:].rearrange("p (c d) -> p c d", c=2),
                               ACT.Copy).then_inc(dn_cp, 1)

            first_rsqrt(0, 0)
            normalise(0, work, x_sb, 0)
            first_rsqrt(1, TB)
            for k in range(KC):
                act.wait_ge(xnT_ps, k + 1)
                act.activation(xnT[:, k, 0, 1:T + 1], bank[k][:], ACT.Copy).then_inc(xnT_act, 1)
            normalise(1, work, x_sb, TB)
            act.wait_ge(consts, 4)
            gate_z(0)
            first_inv(0)
            act.wait_ge(xnT_ps, 4)
            act.activation(xnT[:, 1, 1, 1:T + 1], bank[3][:], ACT.Copy).then_inc(xnT_act, 1)
            gate_z(1)
            gate_r(0)
            gate_r(1)
            first_inv(1)
            for b in range(B):
                first_rsqrt(2 + 2 * b, TB * b)
                normalise(2 + 2 * b, work, work, TB * b)
                if b == 1:
                    copy_down(0)
                first_rsqrt(3 + 2 * b, TB * b)
                normalise(3 + 2 * b, x2n, x_sb, TB * b)
                if b == 1:
                    copy_down(1)
                act.wait_ge(x2T_ps, 2 * b + 2)
                act.activation(x2nT[:, 1, T * b:T * b + T], x2T_b[b][1][:], ACT.Copy).then_inc(x2T_act, 1)
                if b == 0:
                    gate_r(2)
                    gate_r(3)
                    for n in range(3):
                        gate_silu(n)
            for h in range(2):
                cs = slice(TB * h, TB * h + TB)
                act.wait_ge(lg_sub, h + 1)
                act.activation(prob[:, cs, :], below[:, cs, 0:E], ACT.Exp).then_inc(lg_exp, 1)
            for n in range(3, 6):
                gate_silu(n)
            for k in range(2, 4):
                copy_down(k)
            left_over = []

            def step(i, c):
                s = TURN * i + c
                if exists(i, c + 1):
                    act.wait_ge(tx_ps, s + 2)
                    if later(i, c, 1):
                        act.wait_ge(h_ps, s)
                    act.activation(xT[:, (c + 1) % 2, :, :], x_b[:, 0:C].rearrange(
                        "p (k t) -> p k t", k=KC), ACT.Copy).then_inc(xT_done, 1)
                if exists(i, c):
                    act.wait_ge(h_ps, s + 1)
                    if later(i, c, 2):
                        act.wait_ge(hT_ps, s - 1)
                    act.activation(hS[:, c % 2, :], h_b[c % 2][:, 0:I], ACT.Silu).then_inc(h_done, 1)
                if exists(i, c - 2):
                    e = s - 2
                    act.wait_ge(y_ps, e + 1)
                    if later(i, c, 10):
                        act.wait_ge(scat[acc_of(i, c - 10)], added(i, c - 10) + 16)
                    act.wait_ge(sum_done, 4 * i + (c - 2) // 4 + 1)
                    act.activation(yS[:, (c - 2) % 8, :], y_b[c % 2][:, 0:C], ACT.Copy,
                                   scale=slot_sum[:, ((c - 2) // 4) % 4, (c - 2) % 4, 1:2]).then_inc(y_done, 1)
                if isinstance(i, int) and s == LAST - 4:
                    act.wait_ge(ext_done, 1)
                    left_over.append(act.value_load(ext_i[0:1, EXTRA:EXTRA + 1], min_val=0, max_val=1))

            pipeline(act, step)
            with act.If(left_over[0]):
                with act.Fori(0, E * NT) as n:
                    act.wait_ge(o_h_ps, n + 1)
                    act.activation(hS[:, 0, :], h_b[0][:, 0:I], ACT.Silu).then_inc(o_h, 1)
            for h in range(2):
                first_rsqrt(6 + h, TB * h)
                normalise(6 + h, work, work, TB * h)

        @block.tensor
        def _(pe):
            def turn(b, src, dst):
                for k in range(KC):
                    for j in range(TB):
                        mm = pe.transpose(dst[k][:, P * j:P * j + P], src[:, TB * b + j, P * k:P * k + P], ident[:])
                    yield mm

            def product_z(b):
                for m in range(2):
                    for k in range(2 * KC):
                        late = k // KC
                        mm = pe.matmul(bank[4 + 2 * b + m][:], wact_sb[:, k, m, :], xnT[:, k % KC, b, late:late + T],
                                       start=(k == 0), stop=(k == 2 * KC - 1))
                    mm.then_inc(z_ps, 1)

            def product_r(n):
                for c in (2 * n, 2 * n + 1):
                    b, j = c // TB, c % TB
                    for k in range(2 * KC):
                        at = P * j + k // KC
                        mm = pe.matmul(bank[n][:, C * (c % 2):C * (c % 2) + C], xnT[:, k % KC, b, at:at + P],
                                       wrec_sb[:, k, :], start=(k == 0), stop=(k == 2 * KC - 1))
                mm.then_inc(r_ps, 1)

            def product_v(b):
                for c in range(TB * b, TB * b + TB):
                    for m in range(2):
                        mm = pe.matmul(bank[4 + c // 2][:, C * (c % 2):C * (c % 2) + C],
                                       Z[:, m, b, P * (c % TB):P * (c % TB) + P], wval_sb[:, m, :],
                                       start=(m == 0), stop=(m == 1))
                    if c % 2:
                        mm.then_inc(v_ps, 1)

            def logits(b):
                for c in range(TB * b, TB * b + TB):
                    for k in range(KC):
                        mm = pe.matmul(bank[4][:, E * c:E * c + E], x2nT[:, k, P * c:P * c + P], gate_sb[:, k, :],
                                       start=(k == 0), stop=(k == KC - 1))
                mm.then_inc(lg_ps, 1)

            def down(k):
                for c in (2 * k, 2 * k + 1):
                    for j, (_, rows) in enumerate(SC):
                        w = sda_sb[:, j, :] if j < 2 else sdb_sb[:]
                        mm = pe.matmul(dn_b[k][:, C * (c % 2):C * (c % 2) + C],
                                       hidT[0:rows, j, P * c:P * c + P], w, start=(j == 0), stop=(j == 2))
                mm.then_inc(dn_ps, 1)

            def gate_up(n):
                half, (at, rows) = n // 3, SC[n % 3]
                if n == 0:
                    pe.wait_ge(w_in["sgu"], 16)
                if n >= 2:
                    pe.wait_ge(gu_mul, n - 1)
                for g in range(2):
                    for k in range(KC):
                        mm = pe.matmul(bank[2 * (n % 2) + g][0:rows, :], sgu_sb[:, k, IS * g + at:IS * g + at + rows],
                                       x2nT[:, k, T * half:T * half + T], start=(k == 0), stop=(k == KC - 1))
                mm.then_inc(gu_ps, 1)

            def tables(i, c):
                e = TURN * i + c
                pe.wait_ge(hit_done, 2 * e + 2)
                if c % 4 == 0 and later(i, c, 4):
                    pe.wait_ge(sum_done, 4 * i + c // 4)
                at = RC * (c % 4)
                for t in range(NT):
                    mm = pe.matmul(tab_b[:, at:at + RC], hit[:, c % 2, :, t], tslice[:, c % 2, t, :],
                                   start=(t == 0), stop=(t == NT - 1))
                mm.then_inc(tab_ps, 1)

            pe.wait_ge(consts, 8)
            pe.wait_ge(norm_dve, 2)
            pe.wait_ge(norm_act, 2)
            for mm in turn(0, work, bank[0:2]):
                mm.then_inc(xnT_ps, 1)
            pe.wait_ge(w_in["wact"], 16)
            pe.wait_ge(xnT_act, 2)
            product_z(0)
            pe.wait_ge(norm_dve, 4)
            pe.wait_ge(norm_act, 4)
            for mm in turn(1, work, bank[2:4]):
                mm.then_inc(xnT_ps, 1)
            pe.wait_ge(xnT_dve, 1)
            pe.wait_ge(xnT_act, 3)
            product_z(1)
            pe.wait_ge(w_in["wrec"], 16)
            for n in range(3):
                product_r(n)
            pe.wait_ge(w_in["wval"], 16)
            pe.wait_ge(kv_done, 1)
            pe.wait_ge(z_th, 2)
            product_v(0)
            product_r(3)
            pe.wait_ge(r_th, 2)
            pe.wait_ge(norm_dve, 8)
            pe.wait_ge(norm_act, 8)
            for mm in turn(0, x2n, x2T_b[0]):
                mm.then_inc(x2T_ps, 1)
            pe.wait_ge(w_in["gate"], 16)
            pe.wait_ge(x2T_dve, 1)
            pe.wait_ge(x2T_act, 1)
            pe.wait_ge(y_mul, 2)
            logits(0)
            pe.wait_ge(r_th, 4)
            for n in range(3):
                gate_up(n)
            pe.wait_ge(kv_done, 2)
            pe.wait_ge(z_th, 4)
            product_v(1)
            pe.wait_ge(w_in["sda"], 16)
            pe.wait_ge(w_in["sdb"], 16)
            pe.wait_ge(gu_mul, 3)
            down(0)
            down(1)
            pe.wait_ge(norm_dve, 12)
            pe.wait_ge(norm_act, 12)
            pe.wait_ge(y_mul, 4)
            for mm in turn(1, x2n, x2T_b[1]):
                mm.then_inc(x2T_ps, 1)
            pe.wait_ge(x2T_dve, 2)
            pe.wait_ge(x2T_act, 2)
            pe.wait_ge(lg_sub, 1)
            logits(1)
            gate_up(3)
            pe.wait_ge(mask_done, 2)
            pe.matmul(bank[6][:], tri[:], mask[:].rearrange("p c e -> p (c e)"), start=True, stop=False)
            for t in range(1, NT):
                mm = pe.matmul(bank[6][:, E * t:], ones[:], mask[:, 0:NT - t, :].rearrange("p c e -> p (c e)"),
                               start=False, stop=(t == NT - 1))
            mm.then_inc(rank_ps, 1)
            pe.wait_ge(dn_cp, 2)
            gate_up(4)
            for t in range(NT):
                mm = pe.matmul(bank[7][:, 0:E], ones[:], mask[:, t, :], start=(t == 0), stop=(t == NT - 1))
            mm.then_inc(rank_ps, 1)
            for e in range(4):
                tables(0, e)
            gate_up(5)
            for e in range(4, 8):
                tables(0, e)
            pe.wait_ge(gu_mul, 6)
            down(2)
            down(3)
            pe.wait_ge(rank_read, 2)

            def hidden(dst, xTe, w):
                for k in range(KC):
                    mm = pe.matmul(dst, xTe[:, k, :], w[:, I * k:I * k + I], start=(k == 0), stop=(k == KC - 1))
                return mm

            def turn_hidden(dst, h):
                pe.transpose(dst[:, 0:P], h[:, 0:P], ident[:])
                return pe.transpose(dst[0:IR, P:2 * P], h[:, P:I], ident[:])

            def output(dst, hTe, w, wr):
                pe.matmul(dst, hTe[:, 0, :], w[:, KC * I:KC * I + C], start=True, stop=False)
                return pe.matmul(dst, hTe[0:IR, 1, :], wr, start=False, stop=True)

            def step(i, c):
                s = TURN * i + c
                if exists(i, c + 1):
                    e, u = s + 1, c + 1
                    pe.wait_ge(gath[u % 8], 32 * i + 16 * (u // 8 + 1))
                    if later(i, c, 0):
                        pe.wait_ge(xT_done, s + 1)
                    for k in range(KC):
                        mm = pe.transpose(x_b[:, P * k:P * k + P],
                                          xg[:, u % 8, P * k:P * k + P], ident[:])
                    mm.then_inc(tx_ps, 1)
                if exists(i, c):
                    if isinstance(i, int) and s >= E:
                        pe.wait_ge(wld_ext[s - E], 32)
                    else:
                        pe.wait_ge(wld[(c // 2) % 4], 64 * i + 32 * (c // 8 + 1))
                    pe.wait_ge(xT_done, s + 1)
                    if later(i, c, 2):
                        pe.wait_ge(h_done, s - 1)
                    hidden(h_b[c % 2][:, 0:I], xT[:, c % 2], w12_sb[:, c % 8]).then_inc(h_ps, 1)
                if exists(i, c - 1):
                    u = c - 1
                    pe.wait_ge(h_done, s)
                    if later(i, c, 3):
                        pe.wait_ge(hT_done, s - 2)
                    turn_hidden(hT_b[u % 2][:, 0:2 * P], hS[:, u % 2]).then_inc(hT_ps, 1)
                if exists(i, c - 2):
                    u = c - 2
                    pe.wait_ge(hT_done, s - 1)
                    if not later(i, c, 3):
                        pe.wait_ge(dn_cp, 4)
                    if later(i, c, 4):
                        pe.wait_ge(y_done, s - 3)
                    output(y_b[u % 2][:, 0:C], hT[:, u % 2], w12_sb[:, u % 8], w2b_sb[:, u % 8, :]).then_inc(y_ps, 1)
                if has_table(i, c + 9):
                    tables(i, c + 9)

            pipeline(pe, step)
            pe.wait_ge(ext_done, 1)
            with pe.If(pe.value_load(ext_i[0:1, EXTRA:EXTRA + 1], min_val=0, max_val=1)):
                with pe.Fori(0, E * NT) as n:
                    pe.wait_ge(o_x, n + 1)
                    hidden(h_b[0][:, 0:I], xT[:, 0], ow12).then_inc(o_h_ps, 1)
                    pe.wait_ge(o_h, n + 1)
                    turn_hidden(hT_b[0][:, 0:2 * P], hS[:, 0]).then_inc(o_t_ps, 1)
                    pe.wait_ge(o_t, n + 1)
                    output(y_b[0][:, 0:C], hT[:, 0], ow12, ow2b).then_inc(o_y_ps, 1)

        @block.vector
        def _(dve):
            count = [0]

            def mark(ins):
                count[0] += 1
                ins.then_inc(d, 1)

            def settle():
                dve.wait_ge(d, count[0])

            def link(ins):
                mark(ins)
                settle()

            def stats_of(src, cs):
                for c in cs:
                    mark(dve.bn_stats(stats[:, c, :], src[:, c, :]))
                settle()
                for c in cs:
                    mark(dve.bn_aggr(mv[:, c, :], stats[:, c, :]))

            def variances(c0):
                settle()
                cs = slice(c0, c0 + TB)
                dve.tensor_scalar(ve[:, cs], mv[:, cs, 1], EPS, None, ALU.add).then_inc(var_done, 1)

            def sharpen(q, c0):
                cs = slice(c0, c0 + TB)
                dve.wait_ge(rs_act, q + 1)
                link(dve.scalar_tensor_tensor(nt0[:, cs], rs0[:, cs], -0.5, rs0[:, cs], ALU.mult, ALU.mult))
                link(dve.tensor_tensor(nt1[:, cs], nt0[:, cs], ve[:, cs], ALU.mult))
                dve.scalar_tensor_tensor(rstd[:, cs], nt1[:, cs], 1.5, rs0[:, cs], ALU.add, ALU.mult
                                         ).then_inc(rstd_done, 1)
                dve.wait_ge(rstd_done, q + 1)
                dve.scalar_tensor_tensor(shift[:, cs], mv[:, cs, 0], -1.0, rstd[:, cs], ALU.mult, ALU.mult
                                         ).then_inc(shift_done, 1)

            def normalise(q, dst, src, c0):
                for c in (c0, c0 + 1):
                    dve.tensor_scalar(dst[:, c, :], src[:, c, :], mv[:, c, 0:1], rstd[:, c:c + 1],
                                      ALU.subtract, ALU.mult).then_inc(norm_dve, 1)

            for b in range(B):
                for k in (2 * b, 2 * b + 1):
                    dve.wait_ge(x_in[k], 16)
                    stats_of(x_sb, (2 * k, 2 * k + 1))
                variances(TB * b)
                sharpen(b, TB * b)
                normalise(b, work, x_sb, TB * b)
            dve.wait_ge(xnT_ps, 3)
            dve.tensor_copy(xnT[:, 0, 1, 1:T + 1], bank[2][:]).then_inc(xnT_dve, 1)

            def running_max(b):
                dve.wait_ge(mag_done, b + 1)
                dve.tensor_tensor_scan(peak[:, b, :], mag2[:, b, :], mag2[:, b, :], 0.0, ALU.max, ALU.max).then_inc(pk, 1)

            def scale_z(b):
                for m in range(2):
                    mark(dve.scalar_tensor_tensor(Z[:, m, b, :], Z[:, m, b, :], 1.0, inv[:, b, :], ALU.add, ALU.mult))
                settle()

            UP = (1, 2, 4, 8)
            assert T % (2 * UP[-1]) == 0

            def multiply(hi, lo):
                n = hi.shape[2]
                pr, pi = (prod[:, k, 0:2 * n].rearrange("p (m n) -> p m n", m=2) for k in range(2))
                mark(dve.tensor_tensor(pr, lo[:, 0:1].to_broadcast([P, 2, n]), hi, ALU.mult))
                link(dve.tensor_tensor(pi, lo[:, 1:2].to_broadcast([P, 2, n]), hi[:, ::-1], ALU.mult))
                mark(dve.tensor_tensor(hi[:, 0], pr[:, 0], pi[:, 0], ALU.subtract))
                link(dve.tensor_tensor(hi[:, 1], pr[:, 1], pi[:, 1], ALU.add))

            def level(b, first, dist):
                multiply(Z[:, :, b, first:T:2 * dist], Z[:, :, b, first - dist:T - dist:2 * dist])

            def scan_up(b):
                for dist in UP:
                    level(b, 2 * dist - 1, dist)

            def scan_blocks(b):
                step = 2 * UP[-1]
                dist = step
                while dist < T:
                    multiply(Z[:, :, b, step - 1 + dist:T:step], Z[:, :, b, step - 1:T - dist:step])
                    dist *= 2

            def gate_up(n):
                half, rows = n // 3, SC[n % 3][1]
                dve.wait_ge(gu_sil, n + 1)
                dve.tensor_tensor(hidT[0:rows, n % 3, T * half:T * half + T], gsil[0:rows, n % 2, :],
                                  bank[2 * (n % 2) + 1][0:rows, :], ALU.mult).then_inc(gu_mul, 1)

            def residual(b):
                c0 = TB * b
                for k in range(2 * b, 2 * b + 2):
                    dve.wait_ge(v_ps, k + 1)
                    dve.wait_ge(r4_done, k + 1)
                    dve.tensor_tensor(work[:, 2 * k:2 * k + 2, :], bank[4 + k][:].rearrange("p (c d) -> p c d", c=2),
                                      r4[:, 2 * k:2 * k + 2, :], ALU.mult).then_inc(y_mul, 1)
                    dve.wait_ge(y_mul, k + 1)
                    stats_of(work, (2 * k, 2 * k + 1))
                variances(c0)
                sharpen(2 + 2 * b, c0)
                normalise(2 + 2 * b, work, work, c0)
                for done, cs in ((norm_dve, slice(c0, c0 + 2)), (norm_act, slice(c0 + 2, c0 + 4))):
                    dve.wait_ge(done, 2 * (3 + 2 * b))
                    link(dve.tensor_tensor(x_sb[:, cs, :], x_sb[:, cs, :], work[:, cs, :], ALU.add))
                    stats_of(x_sb, (cs.start, cs.start + 1))
                variances(c0)
                sharpen(3 + 2 * b, c0)
                normalise(3 + 2 * b, x2n, x_sb, c0)

            def columns(b):
                dve.wait_ge(x2T_ps, 2 * b + 1)
                dve.tensor_copy(x2nT[:, 0, T * b:T * b + T], x2T_b[b][0][:]).then_inc(x2T_dve, 1)

            lg = bank[4][:].rearrange("p (c e) -> p c e", c=NT)
            tb = table[:, 0:E, :, :].rearrange("p e c n -> p c e n")

            def below_max(h):
                cs = slice(TB * h, TB * h + TB)
                dve.wait_ge(lg_ps, h + 1)
                link(dve.tensor_reduce(lmax[:, cs], lg[:, cs, :], AX.X, ALU.max))
                dve.wait_ge(consts, 17)
                dve.tensor_tensor(below[:, cs, 0:E], lg[:, cs, :], lmax[:, cs].unsqueeze(2).to_broadcast([P, TB, E]),
                                  ALU.subtract).then_inc(lg_sub, 1)

            def choose(h):
                cs = range(TB * h, TB * h + TB)
                dve.wait_ge(lg_sub, h + 1)
                for c in cs:
                    mark(dve.max(top8[:, c, :], below[:, c, :]))
                settle()
                for c in cs:
                    mark(dve.match_replace(left[:, c, :], top8[:, c, :], below[:, c, :], 4.0))
                settle()
                dve.tensor_scalar(mask[:, cs.start:cs.stop, :], left[:, cs.start:cs.stop, 0:E], 3.0, None, ALU.is_gt
                                  ).then_inc(mask_done, 1)

            def weigh(h):
                cs = slice(TB * h, TB * h + TB)
                dve.wait_ge(mask_done, h + 1)
                dve.wait_ge(lg_exp, h + 1)
                link(dve.tensor_tensor(cw[:, cs, :], prob[:, cs, :], mask[:, cs, :], ALU.mult))
                link(dve.tensor_reduce(wsum[:, cs], cw[:, cs, :], AX.X, ALU.add))
                link(dve.reciprocal(wnorm[:, cs], wsum[:, cs]))
                link(dve.tensor_tensor(cw[:, cs, :], cw[:, cs, :], wnorm[:, cs].unsqueeze(2).to_broadcast([P, TB, E]),
                                       ALU.mult))
                link(dve.tensor_copy(tb[:, cs, :, 3], cw[:, cs, :]))
                link(dve.tensor_tensor(left[:, cs, 0:E], cw[:, cs, :], tb[:, cs, :, 3], ALU.subtract))
                link(dve.tensor_copy(tb[:, cs, :, 4], left[:, cs, 0:E]))
                link(dve.tensor_tensor(tb[:, cs, :, 5], left[:, cs, 0:E], tb[:, cs, :, 4], ALU.subtract))

            dve.wait_ge(z_sq, 2)
            dve.tensor_tensor(mag2[:, 0, :], sq[:, 0, 0, :], sq[:, 1, 0, :], ALU.add).then_inc(mag_done, 1)
            running_max(0)
            dve.wait_ge(inv_act, 1)
            dve.wait_ge(pk, 1)
            link(dve.scalar_tensor_tensor(mag2[:, 0, :], inv[:, 0, :], -0.5, inv[:, 0, :], ALU.mult, ALU.mult))
            link(dve.tensor_tensor(mag2[:, 0, :], mag2[:, 0, :], peak[:, 0, :], ALU.mult))
            link(dve.scalar_tensor_tensor(inv[:, 0, :], mag2[:, 0, :], 1.5, inv[:, 0, :], ALU.add, ALU.mult))
            scale_z(0)
            scan_up(0)
            scan_blocks(0)
            for dist in UP[::-1]:
                level(0, 3 * dist - 1, dist)
            dve.tensor_copy(nt0[:, 0:1], nt0[:, 0:1]).then_inc(kv_done, 1)
            running_max(1)
            residual(0)
            columns(0)
            dve.wait_ge(newton, 4)
            scale_z(1)
            scan_up(1)
            scan_blocks(1)
            gate_up(0)
            for dist in UP[::-1]:
                level(1, 3 * dist - 1, dist)
                if dist == 2:
                    gate_up(1)
            dve.tensor_copy(nt0[:, 0:1], nt0[:, 0:1]).then_inc(kv_done, 1)
            gate_up(2)
            residual(1)
            below_max(0)
            columns(1)
            choose(0)
            weigh(0)
            below_max(1)
            choose(1)
            weigh(1)
            gate_up(3)
            dve.wait_ge(rank_ps, 1)
            link(dve.scalar_tensor_tensor(rank1[:, 0:E, :].rearrange("p e c -> p c e"),
                                          bank[6][:].rearrange("p (c e) -> p c e", c=NT), 1.0, mask[:],
                                          ALU.add, ALU.mult))
            link(dve.tensor_scalar(table[:, 0:E, :, 2], rank1[:, 0:E, :], -1.0, 1.0, ALU.mult, ALU.add))

            def hits(i, c):
                e = TURN * i + c
                if later(i, c, 2):
                    dve.wait_ge(tab_ps, e - 1)
                dve.tensor_tensor(hit[:, c % 2], rank1[:, bass.ds(e, 1), :].to_broadcast([P, SLOTS, NT]), slot_no[:],
                                  ALU.is_equal).then_inc(hit_done, 1)
                dve.tensor_copy(tslice[:, c % 2], table[:, bass.ds(e, 1)].rearrange("p e c n -> p (e c) n")
                                ).then_inc(hit_done, 1)

            def sums(i, c):
                e, r = TURN * i + c, (c // 4) % 4
                dve.wait_ge(tab_ps, e + 1)
                if later(i, c, 16):
                    dve.wait_ge(tx_ps, e - 15)
                    dve.wait_ge(y_done, e - 15)
                    for u in range(c - c % 4 - 16, c - c % 4 - 12):
                        dve.wait_ge(scat[acc_of(i, u)], added(i, u) + 16)
                dve.tensor_reduce(slot_sum[:, r], tab_b[:, 0:4 * RC].rearrange(
                    "p (e q n) -> p e q n", e=4, q=2), AX.X, ALU.add).then_inc(sum_done, 1)
                dve.wait_ge(sum_done, 4 * i + c // 4 + 1)
                dve.tensor_scalar(gat_idx[:, r], slot_sum[:, r, :, 0], trash_no[:, 0:1], None, ALU.add
                                  ).then_inc(idx_done, 1)

            for e in range(4):
                hits(0, e)
            sums(0, 3)
            for e in range(4, 6):
                hits(0, e)
            gate_up(4)
            dve.scalar_tensor_tensor(rank_f[:], bank[6][:].rearrange("p (c e) -> p c e", c=NT), 1.0, mask[:],
                                     ALU.add, ALU.mult).then_inc(rank_read, 1)
            dve.wait_ge(rank_ps, 2)
            dve.tensor_scalar(full_i[:], bank[7][:, 0:E], float(SLOTS - 1), None, ALU.add).then_inc(rank_read, 1)
            hits(0, 6)
            gate_up(5)
            hits(0, 7)
            sums(0, 7)
            left_over = []

            shape = [P, EXTRA, E]
            before_b, upto_b = before[:].unsqueeze(1).to_broadcast(shape), upto[:].unsqueeze(1).to_broadcast(shape)

            def count_blocks():
                dve.wait_ge(rank_read, 2)
                link(dve.tensor_scalar(full_i[:], full_i[:], 7, None, ALU.arith_shift_right))
                link(dve.tensor_scalar(full[:], full_i[:], -1.0, 0.0, ALU.add, ALU.max))
                link(dve.tensor_tensor_scan(upto[:], full[:], zeros[:, 0:E], 0.0, ALU.add, ALU.add))
                link(dve.tensor_tensor(before[:], upto[:], full[:], ALU.subtract))

            def find_experts():
                mark(dve.tensor_tensor(ext_a[:], before_b, ext_no[:], ALU.is_le))
                link(dve.tensor_tensor(ext_b[:], upto_b, ext_no[:], ALU.is_gt))
                link(dve.tensor_tensor(ext_a[:], ext_a[:], ext_b[:], ALU.mult))
                link(dve.tensor_tensor(ext_b[:], ext_a[:], ext_e[:], ALU.mult))
                link(dve.tensor_reduce(ext_s[:, 0, :], ext_b[:], AX.X, ALU.add))

            def find_slots():
                link(dve.scalar_tensor_tensor(ext_b[:], before_b, float(NT), ext_no[:], ALU.add, ALU.subtract))
                link(dve.tensor_tensor(ext_b[:], ext_a[:], ext_b[:], ALU.mult))
                link(dve.tensor_reduce(ext_s[:, 1, :], ext_b[:], AX.X, ALU.add))
                link(dve.tensor_scalar(ext_s[:, 1, :], ext_s[:, 1, :], float(SLOTS), -float(NTOK + SLOTS),
                                       ALU.mult, ALU.add))

            def publish():
                mark(dve.tensor_copy(ext_i[:, 0:EXTRA], ext_s[:, 0, :]))
                link(dve.tensor_scalar(ext_i[:, EXTRA:], upto[:, E - 1:E], float(EXTRA), None, ALU.is_gt))
                dve.tensor_copy(nt0[:, 0:1], ext_s[:, 0, 0:1]).then_inc(ext_done, 1)

            def fill_block(n):
                e = dve.value_load(ext_i[0:1, n:n + 1], min_val=0, max_val=E - 1)
                mark(dve.tensor_scalar(rank1[:, E + n:E + n + 1, :], rank_f[:, :, bass.ds(e, 1)].rearrange("p c e -> p e c"),
                                       ext_s[:, 1, n:n + 1], None, ALU.add))
                link(dve.tensor_copy(table[:, E + n:E + n + 1], table[:, bass.ds(e, 1)]))
                link(dve.tensor_scalar(table[:, E + n, :, 2], rank1[:, E + n, :], -1.0, 1.0, ALU.mult, ALU.add))

            assert EXTRA == 2

            def step(i, c):
                s = TURN * i + c
                if has_table(i, c + 9):
                    hits(i, c + 9)
                if exists(i, c - 1):
                    dve.wait_ge(hT_ps, s)
                    if later(i, c, 3):
                        dve.wait_ge(y_ps, s - 2)
                    u = (c - 1) % 2
                    dve.tensor_copy(hT[:, u].rearrange("p k t -> p (k t)"), hT_b[u][:, 0:2 * P]
                                    ).then_inc(hT_done, 1)
                if later(i, c, 0) and has_table(i, c + 8) and (c % 4 == 3 or not has_table(i, c + 9)):
                    sums(i, c + 8)
                if isinstance(i, int):
                    if s == 0:
                        count_blocks()
                    elif s == 1:
                        find_experts()
                    elif s == 2:
                        find_slots()
                    elif s == 3:
                        publish()
                    elif s in (5, 6):
                        fill_block(s - 5)
                    elif s == LAST - 4:
                        left_over.append(dve.value_load(ext_i[0:1, EXTRA:EXTRA + 1], min_val=0, max_val=1))

            pipeline(dve, step)

            with dve.If(left_over[0]):
                for q in range(4):
                    dve.wait_ge(fin_in[q], 32)
                block_i = left[:, :, 0:E].bitcast(I32)
                dve.tensor_scalar(block_i, rank_f[:], float(SLOTS - 1), None, ALU.add).then_inc(o_cw, 1)
                dve.wait_ge(o_cw, 1)
                dve.tensor_scalar(block_i, block_i, 7, None, ALU.arith_shift_right).then_inc(o_cw, 1)
                dve.wait_ge(o_cw, 2)
                dve.tensor_copy(rank_f[:], block_i).then_inc(o_cw, 1)
                dve.wait_ge(o_cw, 3)
                dve.scalar_tensor_tensor(cw[:], rank_f[:], 1.5, cw[:], ALU.is_gt, ALU.mult).then_inc(o_cw, 1)
                dve.wait_ge(o_cw, 4)
                dve.tensor_tensor(rank_f[:], rank_f[:], before[:].unsqueeze(1).to_broadcast([P, NT, E]),
                                  ALU.add).then_inc(o_cw, 1)
                dve.wait_ge(o_cw, 5)
                dve.scalar_tensor_tensor(over_cw, rank_f[:], EXTRA + 1.5, cw[:], ALU.is_gt, ALU.mult).then_inc(o_y, 1)
                with dve.Fori(0, E) as e:
                    dve.wait_ge(o_y, e * NT + 1)
                    dve.wait_ge(o_ld, 32 * e + 32)
                    for c in range(NT):
                        n = e * NT + c
                        dve.tensor_copy(xT[:, 0], x2nT[:, :, P * c:P * c + P]).then_inc(o_x, 1)
                        dve.wait_ge(o_t_ps, n + 1)
                        dve.tensor_copy(hT[:, 0].rearrange("p k t -> p (k t)"), hT_b[0][:, 0:2 * P]).then_inc(o_t, 1)
                        dve.wait_ge(o_y_ps, n + 1)
                        dve.scalar_tensor_tensor(work[:, c, :], y_b[0][:, 0:C], over_cw[:, c, bass.ds(e, 1)],
                                                 work[:, c, :], ALU.mult, ALU.add).then_inc(o_y, 1)
                dve.wait_ge(o_y, E * NT + 1)

            for h in range(2):
                for q in (2 * h, 2 * h + 1):
                    cs = slice(2 * q, 2 * q + 2)
                    dve.wait_ge(fin_in[q], 32)
                    link(dve.tensor_tensor(work[:, cs, :], work[:, cs, :], part[3][:, cs, :], ALU.add))
                    dve.wait_ge(sum_pool, q + 1)
                    link(dve.tensor_tensor(work[:, cs, :], work[:, cs, :], part[2][:, cs, :], ALU.add))
                    stats_of(work, (2 * q, 2 * q + 1))
                variances(TB * h)
            for h in range(2):
                sharpen(6 + h, TB * h)
                normalise(6 + h, work, work, TB * h)
            for k in (2, 3):
                cs = slice(2 * k, 2 * k + 2)
                dve.wait_ge((norm_dve, norm_act)[k - 2], 16)
                dve.tensor_tensor(work[:, cs, :], work[:, cs, :], x_sb[:, cs, :], ALU.add).then_inc(fin_dve, 1)


def kernel(L0_attn_x, L0_attn_W_act, L0_attn_W_val, L0_attn_W_rec, L0_ffn_gate_w, L0_ffn_experts_w1,
           L0_ffn_experts_w2, L0_ffn_shared_gate_up, L0_ffn_shared_down):
    import numpy as np
    import concourse.bacc as bacc
    from concourse.bass_utils import run_bass_kernel_spmd

    x = np.asarray(L0_attn_x)
    bx, tx, C = x.shape
    KC = C // P
    E, I, _ = L0_ffn_experts_w1.shape
    IS = L0_ffn_shared_down.shape[1]

    def by_k(w):
        w = np.asarray(w)
        return w.T.reshape(w.shape[1] // P, P, w.shape[0]).transpose(1, 0, 2)

    w_act = by_k(L0_attn_W_act).reshape(P, 2 * KC, C // 2, 2).transpose(0, 1, 3, 2)
    w_val = np.asarray(L0_attn_W_val).T.reshape(C // 2, 2, C)
    w1 = np.asarray(L0_ffn_experts_w1).transpose(0, 2, 1).reshape(E, KC, P, I).transpose(0, 2, 1, 3).reshape(E, P, KC * I)
    w2 = np.asarray(L0_ffn_experts_w2).transpose(0, 2, 1)
    sd = np.asarray(L0_ffn_shared_down).T
    arrays = {
        "x": x.reshape(bx * tx, C),
        "w_act": w_act,
        "w_rec": by_k(L0_attn_W_rec),
        "w_val": w_val,
        "gate": by_k(L0_ffn_gate_w),
        "w12": np.concatenate([w1, w2[:, 0:P, :]], axis=2),
        "w2b": w2[:, P:, :],
        "sgu": by_k(L0_ffn_shared_gate_up),
        "sd_a": sd[0:2 * P].reshape(2, P, C).transpose(1, 0, 2),
        "sd_b": sd[2 * P:],
    }
    arrays = {n: np.ascontiguousarray(a) for n, a in arrays.items()}
    nc = bacc.Bacc("TRN2", target_bir_lowering=False, num_devices=1)
    aps = {n: nc.dram_tensor(n, a.shape, F32, kind="ExternalInput").ap() for n, a in arrays.items()}
    out = nc.dram_tensor("out", (bx * tx, C), F32, kind="ExternalOutput").ap()
    moe_block(nc, out=out, **aps)
    r = run_bass_kernel_spmd(nc, [arrays], core_ids=[0])
    return r.results[0]["out"].reshape(bx, tx, C)
```

```python
from contextlib import ExitStack

import concourse.bass as bass
from concourse import mybir

F32 = mybir.dt.float32
BF16 = mybir.dt.bfloat16
I32 = mybir.dt.int32
U32 = mybir.dt.uint32
ALU = mybir.AluOpType
ACT = mybir.ActivationFunctionType
AX = mybir.AxisListType

P = 128
EPS = 1e-5
TOPK = 6
SLOTS = P
EXTRA = 2
ACCS = 4


def moe_block(nc, x, w_act, w_rec, w_val, gate, w12, w2b, sgu, sd_a, sd_b, out):
    NTOK, C = x.shape
    NT = NTOK // P
    B = 2
    T = NTOK // B
    TB = T // P
    KC = C // P
    E = gate.shape[2]
    I = (w12.shape[2] - C) // KC
    IR = I - P
    IS = sgu.shape[2] // 2
    SC = [(0, P), (P, P), (2 * P, IS - 2 * P)]
    NB = E + EXTRA
    RC = 6
    TRASH = P
    AHEAD = 8
    assert NT == 8 and KC == 2 and B == 2 and E % 8 == 0 and 0 < IR <= 64 and len(SC) == 3

    x_rows = nc.dram_tensor("x_rows", [NTOK + TRASH, C], F32).ap()
    acc_rows = [nc.dram_tensor(f"acc_rows{j}", [NTOK + TRASH, C], F32).ap() for j in range(ACCS)]

    with ExitStack() as ctx:
        def sb(name, shape, dt=F32):
            return ctx.enter_context(nc.sbuf_tensor(name, shape, dt))

        def sem(name):
            return ctx.enter_context(nc.semaphore(name))

        bank = [ctx.enter_context(nc.psum_tensor(f"bank{i}", [P, 512], F32)) for i in range(8)]

        ident = sb("ident", [P, P])
        tri = sb("tri", [P, P], BF16)
        ones = sb("ones", [P, P], BF16)
        slot_no = sb("slot_no", [P, SLOTS, NT], BF16)
        trash_no = sb("trash_no", [P, 1])
        zeros = sb("zeros", [P, C])
        half_one = sb("half_one", [P, 2])
        pace = sb("pace", [P, 1])
        wact_sb = sb("wact_sb", [P, 2 * KC, 2, P])
        wrec_sb = sb("wrec_sb", [P, 2 * KC, C])
        wval_sb = sb("wval_sb", [P, 2, C])
        gate_sb = sb("gate_sb", [P, KC, E])
        sgu_sb = sb("sgu_sb", [P, KC, 2 * IS])
        sda_sb = sb("sda_sb", [P, 2, C])
        sdb_sb = sb("sdb_sb", [SC[2][1], C])
        x_sb = sb("x_sb", [P, NT, C])
        work = sb("work", [P, NT, C])
        work2 = sb("work2", [P, NT, C])
        xnT = sb("xnT", [P, KC, B, T + 1])
        zbuf = sb("zbuf", [P, 2 * B * T])
        Z = zbuf[:].rearrange("p (m b t) -> p m b t", m=2, b=B)
        mag2 = sb("mag2", [P, B, T])
        prod = sb("prod", [P, 2, T])
        prod_pool = sb("prod_pool", [P, 2, T])
        hidT = sb("hidT", [P, 3, NTOK])
        inv = sb("inv", [P, B, T])
        peak = sb("peak", [P, B, T])
        r4 = sb("r4", [P, NT, C])
        x2n = r4
        x2nT = sb("x2nT", [P, KC, NTOK])
        stats = sb("stats", [P, NT, 6])
        mv = sb("mv", [P, NT, 2])
        rstd = sb("rstd", [P, NT])
        shift = sb("shift", [P, NT])
        ve = sb("ve", [P, NT])
        rs0 = sb("rs0", [P, NT])
        nt0 = sb("nt0", [P, NT])
        nt1 = sb("nt1", [P, NT])
        lmax = sb("lmax", [P, NT])
        below = sb("below", [P, NT, E + 2])
        prob = sb("prob", [P, NT, E])
        left = sb("left", [P, NT, E + 2])
        top8 = sb("top8", [P, NT, 8])
        wsum = sb("wsum", [P, NT])
        wnorm = sb("wnorm", [P, NT])
        cw = sb("cw", [P, NT, E])
        mask = sb("mask", [P, NT, E], BF16)
        rank1 = sb("rank1", [P, NB + 1, NT], BF16)
        table = sb("table", [P, NB + 1, NT, RC], BF16)
        rank_f = sb("rank_f", [P, NT, E])
        full = sb("full", [P, E])
        full_i = sb("full_i", [P, E], I32)
        upto = sb("upto", [P, E])
        before = sb("before", [P, E])
        ext_no = sb("ext_no", [P, EXTRA, E])
        ext_e = sb("ext_e", [P, EXTRA, E])
        ext_a = sb("ext_a", [P, EXTRA, E])
        ext_b = sb("ext_b", [P, EXTRA, E])
        ext_s = sb("ext_s", [P, 2, EXTRA])
        ext_i = sb("ext_i", [P, EXTRA + 1], I32)
        over_cw = left[:, :, 0:E]
        hit = sb("hit", [P, 2, SLOTS, NT], BF16)
        tslice = sb("tslice", [P, 2, NT, RC], BF16)
        slot_sum = sb("slot_sum", [P, 4, 4, 2])
        gat_idx = sb("gat_idx", [P, 4, 4], U32)
        w12_sb = sb("w12_sb", [P, 8, w12.shape[2]])
        w2b_sb = sb("w2b_sb", [IR, 8, C])
        xg = sb("xg", [P, 8, C])
        xT = sb("xT", [P, 2, KC, P])
        hS = sb("hS", [P, 2, I])
        hT = sb("hT", [P, 2, 2, P])
        yS = sb("yS", [P, 8, C])
        sq = work2[:].rearrange("p (b h) d -> p b (h d)", b=B).rearrange("p b (m t) -> p m b t", m=2)
        gsil = work2[:, 0:4, :].rearrange("p (a c) d -> p a (c d)", a=2)
        part = (work, work2, zbuf[:].rearrange("p (c d) -> p c d", c=NT),
                x2n)
        y_sh = sb("y_sh", [P, TB, C])
        ow12, ow2b = w12_sb[:, 0, :], w2b_sb[:, 0, :]

        tab_b, x_b, h_b, hT_b, y_b = bank[5], bank[4], (bank[1], bank[6]), (bank[0], bank[7]), bank[2:4]
        x2T_b = ((bank[0], bank[1]), (bank[6], bank[7]))
        dn_b = (bank[5], bank[0], bank[4], bank[5])

        x_in = [sem(f"x_in{k}") for k in range(4)]
        w_in = {n: sem(f"in_{n}") for n in ("wact", "wrec", "wval", "gate", "sgu", "sda", "sdb")}
        consts = sem("consts")
        d = sem("d")
        var_done = sem("var_done")
        rs_act = sem("rs_act")
        rstd_done = sem("rstd_done")
        shift_done = sem("shift_done")
        norm_dve = sem("norm_dve")
        norm_act = sem("norm_act")
        xnT_ps = sem("xnT_ps")
        xnT_act = sem("xnT_act")
        xnT_dve = sem("xnT_dve")
        z_ps = sem("z_ps")
        z_th = sem("z_th")
        z_relu = sem("z_relu")
        z_sq = sem("z_sq")
        mag_done = sem("mag_done")
        pk = sem("pk")
        inv_act = sem("inv_act")
        pool_chain = sem("pool_chain")
        share_done = sem("share_done")
        blocks_done = sem("blocks_done")
        z_plus = sem("z_plus")
        kv_done = sem("kv_done")
        r_ps = sem("r_ps")
        r_th = sem("r_th")
        r_relu = sem("r_relu")
        r_sq = sem("r_sq")
        r4_done = sem("r4_done")
        v_ps = sem("v_ps")
        y_mul = sem("y_mul")
        x2T_ps = sem("x2T_ps")
        x2T_act = sem("x2T_act")
        x2T_dve = sem("x2T_dve")
        lg_ps = sem("lg_ps")
        lg_sub = sem("lg_sub")
        lg_exp = sem("lg_exp")
        mask_done = sem("mask_done")
        rank_ps = sem("rank_ps")
        rank_read = sem("rank_read")
        ext_done = sem("ext_done")
        gu_ps = sem("gu_ps")
        gu_sil = sem("gu_sil")
        gu_mul = sem("gu_mul")
        dn_ps = sem("dn_ps")
        dn_cp = sem("dn_cp")
        xrow_out = sem("xrow_out")
        acc_init = [sem(f"acc_init{j}") for j in range(ACCS)]
        hit_done = sem("hit_done")
        tab_ps = sem("tab_ps")
        sum_done = sem("sum_done")
        idx_done = sem("idx_done")
        paced = sem("paced")
        gath = [sem(f"gath{j}") for j in range(8)]
        wld = [sem(f"wld{j}") for j in range(4)]
        wld_ext = [sem(f"wld_ext{j}") for j in range(EXTRA)]
        tx_ps = sem("tx_ps")
        xT_done = sem("xT_done")
        h_ps = sem("h_ps")
        h_done = sem("h_done")
        hT_ps = sem("hT_ps")
        hT_done = sem("hT_done")
        y_ps = sem("y_ps")
        y_done = sem("y_done")
        scat = [sem(f"scat{j}") for j in range(ACCS)]
        part_in = sem("part_in")
        fin_in1 = [sem(f"fin_in1{q}") for q in range(4)]
        fin_in3 = [sem(f"fin_in3{q}") for q in range(4)]
        fin_in = [sem(f"fin_in{q}") for q in range(4)]
        sh_added = sem("sh_added")
        sum_pool = sem("sum_pool")
        fin_pool = sem("fin_pool")
        fin_dve = sem("fin_dve")
        out_done = sem("out_done")
        o_ld = sem("o_ld")
        o_cw = sem("o_cw")
        o_x = sem("o_x")
        o_h_ps = sem("o_h_ps")
        o_h = sem("o_h")
        o_t_ps = sem("o_t_ps")
        o_t = sem("o_t")
        o_y_ps = sem("o_y_ps")
        o_y = sem("o_y")

        TURN = 16
        HEAD = 10
        LOOPS = (NB - 8 - HEAD) // TURN
        TAIL = HEAD + TURN * LOOPS
        LAST = NB + 1

        def pipeline(engine, step):
            for s in range(-1, HEAD):
                step(0, s)
            with engine.Fori(0, LOOPS) as i:
                for u in range(TURN):
                    step(i, HEAD + u)
            for s in range(TAIL, LAST + 1):
                step(LOOPS, s - TURN * LOOPS)

        assert ACCS == 4
        acc_by_block = [e % ACCS if e < TAIL - 2 else (0, 1, 3)[(e - TAIL + 2) % 3] for e in range(NB)]
        adds = [acc_by_block.count(j) for j in range(ACCS)]

        def acc_of(i, c):
            return acc_by_block[TURN * i + c] if isinstance(i, int) else c % ACCS

        def added(i, c):
            e = TURN * i + c
            return 16 * acc_by_block[:e].count(acc_by_block[e]) if isinstance(i, int) else 64 * i + 16 * (c // ACCS)

        def exists(i, c):
            return not isinstance(i, int) or 0 <= TURN * i + c < NB

        def has_table(i, c):
            return not isinstance(i, int) or TURN * i + c <= NB

        def later(i, c, n):
            return not isinstance(i, int) or TURN * i + c >= n

        UP = (1, 2, 4, 8)
        assert T % (2 * UP[-1]) == 0

        def parts(scratch, n):
            return tuple(scratch[:, k, 0:2 * n].rearrange("p (m n) -> p m n", m=2) for k in range(2))

        def factors(b, first, end, dist, scratch):
            n = (end - 1 - first) // (2 * dist) + 1
            return (Z[:, :, b, first:end:2 * dist], Z[:, :, b, first - dist:end - dist:2 * dist],
                    parts(scratch, n))

        CUT = 13 * T // 16

        block = ctx.enter_context(nc.Block())

        @block.sync
        def _(sp):
            xt = x.rearrange("(c p) d -> p c d", p=P)
            for k in range(4):
                sp.dma_start(x_sb[:, 2 * k:2 * k + 2, :], xt[:, 2 * k:2 * k + 2, :]).then_inc(x_in[k], 16)
            sp.dma_start(wact_sb[:], w_act).then_inc(w_in["wact"], 16)
            sp.dma_start(wrec_sb[:], w_rec).then_inc(w_in["wrec"], 16)
            sp.dma_start(wval_sb[:], w_val).then_inc(w_in["wval"], 16)
            sp.dma_start(gate_sb[:], gate).then_inc(w_in["gate"], 16)
            sp.dma_start(sgu_sb[:], sgu).then_inc(w_in["sgu"], 16)
            sp.dma_start(sda_sb[:], sd_a).then_inc(w_in["sda"], 16)
            sp.dma_start(sdb_sb[:], sd_b).then_inc(w_in["sdb"], 16)

            def rows_of(j, q):
                return acc_rows[j][2 * P * q:2 * P * q + 2 * P, :].rearrange("(c p) d -> p c d", p=P)

            def load_pair(e, j):
                sp.dma_start(w12_sb[:, 2 * j:2 * j + 2, :],
                             w12[bass.ds(e, 2)].rearrange("e p n -> p e n")).then_inc(wld[j], 16)
                sp.dma_start(w2b_sb[:, 2 * j:2 * j + 2, :],
                             w2b[bass.ds(e, 2)].rearrange("e p n -> p e n")).then_inc(wld[j], 16)

            for j in range(4):
                load_pair(2 * j, j)
            sp.wait_ge(consts, 10)
            sp.dma_start(x_rows[NTOK:NTOK + TRASH, :], zeros[:]).then_inc(xrow_out, 16)
            for j in range(ACCS):
                sp.dma_start(acc_rows[j][NTOK:NTOK + TRASH, :], zeros[:]).then_inc(acc_init[j], 16)
                for c in range(0 if j else TB, NT):
                    sp.dma_start(acc_rows[j][P * c:P * c + P, :], zeros[:]).then_inc(acc_init[j], 16)
            xr = x_rows[0:NTOK, :].rearrange("(c p) d -> p c d", p=P)
            for b in range(B):
                sp.wait_ge(norm_dve, 8 + 4 * b)
                sp.wait_ge(norm_act, 8 + 4 * b)
                sp.dma_start(xr[:, TB * b:TB * b + TB, :], x2n[:, TB * b:TB * b + TB, :]).then_inc(xrow_out, 16)
            sp.wait_ge(dn_cp, 2)
            sp.dma_start(acc_rows[0][0:T, :].rearrange("(c p) d -> p c d", p=P), y_sh[:]).then_inc(acc_init[0], 16)
            with sp.Fori(0, E // 8 - 1) as i:
                for j in range(4):
                    sp.wait_ge(y_ps, 8 * i + 2 * j + 2)
                    load_pair(8 * i + 8 + 2 * j, j)
            sp.wait_ge(ext_done, 1)
            for n in range(EXTRA):
                e = sp.value_load(ext_i[0:1, n:n + 1], min_val=0, max_val=E - 1)
                sp.wait_ge(y_ps, E - 8 + n + 1)
                sp.dma_start(w12_sb[:, n, :], w12[bass.ds(e, 1)].rearrange("e p n -> p (e n)")).then_inc(wld_ext[n], 16)
                sp.dma_start(w2b_sb[:, n, :], w2b[bass.ds(e, 1)].rearrange("e p n -> p (e n)")).then_inc(wld_ext[n], 16)
            sp.wait_ge(scat[2], 16 * adds[2])
            for q in range(4):
                sp.wait_ge(y_ps, E - 3 + q)
                sp.dma_start(part[2][:, 2 * q:2 * q + 2, :], rows_of(2, q)).then_inc(part_in, 16)
            for j in (1, 3, 0):
                sp.wait_ge(scat[j], 16 * adds[j])
                if j == 1:
                    for q in range(2):
                        sp.dma_start(part[1][:, 2 * q:2 * q + 2, :], rows_of(1, q)).then_inc(fin_in1[q], 16)
            for q in range(4):
                for j in (1, 3, 0) if q >= 2 else (3, 0):
                    sp.dma_start(part[j][:, 2 * q:2 * q + 2, :], rows_of(j, q)).then_inc(
                        {1: fin_in1, 3: fin_in3, 0: fin_in}[j][q], 16)
            with sp.If(sp.value_load(ext_i[0:1, EXTRA:EXTRA + 1], min_val=0, max_val=1)):
                with sp.Fori(0, E) as e:
                    sp.wait_ge(o_y, e * NT + 1)
                    sp.dma_start(ow12, w12[bass.ds(e, 1)].rearrange("e p n -> p (e n)")).then_inc(o_ld, 16)
                    sp.dma_start(ow2b, w2b[bass.ds(e, 1)].rearrange("e p n -> p (e n)")).then_inc(o_ld, 16)
            outv = out.rearrange("(c p) d -> p c d", p=P)
            for k in range(4):
                if k < 2:
                    sp.wait_ge(fin_pool, k + 1)
                else:
                    sp.wait_ge(fin_dve, k - 1)
                sp.dma_start(outv[:, 2 * k:2 * k + 2, :], work[:, 2 * k:2 * k + 2, :]).then_inc(out_done, 16)
            sp.wait_ge(out_done, 64)

        @block.gpsimd
        def _(pool):
            pool.memset(ident[:], 0.0).then_inc(consts, 1)
            pool.wait_ge(consts, 1)
            pool.affine_select(out=ident[:], in_=ident[:], compare_op=ALU.not_equal, fill=1.0, base=0,
                               pattern=[[-1, P]], channel_multiplier=1).then_inc(consts, 1)
            pool.memset(half_one[:, 0:1], 0.5).then_inc(consts, 1)
            pool.memset(half_one[:, 1:2], 1.0).then_inc(consts, 1)
            pool.memset(zeros[:], 0.0).then_inc(consts, 1)
            pool.memset(ones[:], 1.0).then_inc(consts, 1)
            pool.wait_ge(consts, 6)
            pool.affine_select(out=tri[:], in_=ones[:], compare_op=ALU.is_gt, fill=0.0, base=0,
                               pattern=[[1, P]], channel_multiplier=-1).then_inc(consts, 1)
            pool.memset(xnT[:, :, :, 0:1], 0.0).then_inc(consts, 1)
            pool.iota(slot_no[:], [[1, SLOTS], [0, NT]], base=1, channel_multiplier=0,
                      allow_small_or_imprecise_dtypes=True).then_inc(consts, 1)
            pool.iota(trash_no[:], [[0, 1]], base=NTOK, channel_multiplier=1,
                      allow_small_or_imprecise_dtypes=True).then_inc(consts, 1)
            pool.iota(table[:, 0:E, :, 0], [[0, E], [P, NT]], base=-NTOK, channel_multiplier=0,
                      allow_small_or_imprecise_dtypes=True).then_inc(consts, 1)
            pool.iota(table[:, 0:E, :, 1], [[0, E], [0, NT]], base=0, channel_multiplier=1,
                      allow_small_or_imprecise_dtypes=True).then_inc(consts, 1)
            pool.memset(rank1[:, NB:, :], 0.0).then_inc(consts, 1)
            pool.memset(table[:, NB:, :, :], 0.0).then_inc(consts, 1)
            pool.memset(below[:, :, E:E + 2], 2.0).then_inc(consts, 1)
            pool.iota(ext_no[:], [[1, EXTRA], [0, E]], base=0, channel_multiplier=0,
                      allow_small_or_imprecise_dtypes=True).then_inc(consts, 1)
            pool.iota(ext_e[:], [[0, EXTRA], [1, E]], base=0, channel_multiplier=0,
                      allow_small_or_imprecise_dtypes=True).then_inc(consts, 1)
            steps = [0]

            def mark(ins):
                steps[0] += 1
                ins.then_inc(pool_chain, 1)

            def link(ins):
                mark(ins)
                pool.wait_ge(pool_chain, steps[0])

            def scale(b, t0):
                m, v = mag2[:, b, t0:], inv[:, b, t0:]
                pool.wait_ge(inv_act, b + 1)
                pool.wait_ge(pk, b + 1)
                pool.wait_ge(z_plus, b + 1)
                link(pool.tensor_tensor(m, v, v, ALU.mult))
                link(pool.tensor_tensor(m, m, peak[:, b, t0:], ALU.mult))
                link(pool.tensor_scalar(m, m, -0.5, 1.5, ALU.mult, ALU.add))
                link(pool.tensor_tensor(v, m, v, ALU.mult))
                link(pool.tensor_tensor(Z[:, :, b, t0:], Z[:, :, b, t0:],
                                        inv[:, b:b + 1, t0:].to_broadcast([P, 2, T - t0]), ALU.mult))

            def level(b, first, dist):
                hi, lo, (pr, pi) = factors(b, first, T, dist, prod_pool)
                n = hi.shape[2]
                mark(pool.tensor_tensor(pr, lo[:, 0:1].to_broadcast([P, 2, n]), hi, ALU.mult))
                link(pool.tensor_tensor(pi, lo[:, 1:2].to_broadcast([P, 2, n]), hi[:, ::-1], ALU.mult))
                mark(pool.tensor_tensor(hi[:, 0], pr[:, 0], pi[:, 0], ALU.subtract))
                link(pool.tensor_tensor(hi[:, 1], pr[:, 1], pi[:, 1], ALU.add))

            scale(0, CUT)
            for dist in UP:
                level(0, CUT + 2 * dist - 1, dist)
            pool.tensor_tensor(pace[:, 0:1], trash_no[:], trash_no[:], ALU.add).then_inc(share_done, 1)
            pool.wait_ge(z_sq, 4)
            pool.tensor_tensor(mag2[:, 1, :], sq[:, 0, 1, :], sq[:, 1, 1, :], ALU.add).then_inc(mag_done, 1)
            scale(1, 0)
            for dist in UP:
                level(1, 2 * dist - 1, dist)
            pool.wait_ge(share_done, 1)
            pool.tensor_tensor(pace[:, 0:1], trash_no[:], trash_no[:], ALU.add).then_inc(share_done, 1)
            pool.wait_ge(blocks_done, 1)
            for dist in UP[::-1]:
                level(1, CUT + dist - 1, dist)
            pool.wait_ge(share_done, 2)
            pool.tensor_tensor(pace[:, 0:1], trash_no[:], trash_no[:], ALU.add).then_inc(share_done, 1)
            pool.wait_ge(share_done, 3)
            pool.wait_ge(xrow_out, 48)
            for j in range(1, ACCS):
                pool.wait_ge(acc_init[j], 16 * (NT + 1))

            def await_gather(i, c):
                e = TURN * i + c
                pool.wait_ge(idx_done, 4 * i + c // 4 + 1)
                if later(i, c, 8):
                    pool.wait_ge(tx_ps, e - 7)

            def gather(c):
                pool.indirect_dma_start(xg[:, c % 8, :], None, x_rows, bass.IndirectOffsetOnAxis(
                    ap=gat_idx[:, (c // 4) % 4, c % 4:c % 4 + 1], axis=0)).then_inc(gath[c % 8], 16)

            def await_scatter(i, c):
                e = TURN * i + c
                if later(i, c, ACCS):
                    pool.wait_ge(scat[acc_of(i, c)], added(i, c))
                pool.wait_ge(y_done, e + 1)

            def scatter(i, c):
                pool.indirect_dma_start(acc_rows[acc_of(i, c)], bass.IndirectOffsetOnAxis(
                    ap=gat_idx[:, (c // 4) % 4, c % 4:c % 4 + 1], axis=0), yS[:, c % 8, :], None,
                    compute_op=ALU.add).then_inc(scat[acc_of(i, c)], 16)

            pool.tensor_tensor(pace[:, 0:1], trash_no[:], trash_no[:], ALU.add).then_inc(paced, 1)
            for e in range(3):
                await_gather(0, e)
                gather(e)

            def step(i, c):
                if isinstance(i, int):
                    if exists(i, c + 4):
                        await_gather(i, c + 4)
                        gather(c + 4)
                    s = TURN * i + c
                    if s == 2:
                        pool.wait_ge(acc_init[0], 16 * (TB + 2))
                    for u in {HEAD - 2: (), HEAD - 1: (), TAIL: (c - 4, c - 3, c - 2)}.get(s, (c - 2,)):
                        if exists(i, u):
                            await_scatter(i, u)
                            scatter(i, u)
                elif c % 2 == 0:
                    for u in (c, c + 1):
                        await_gather(i, u + 4)
                        await_scatter(i, u - 4)
                    pool.wait_ge(paced, TURN // 2 * i + (c - HEAD) // 2 + 1)
                    pool.tensor_tensor(pace[:, 0:1], trash_no[:], trash_no[:], ALU.add).then_inc(paced, 1)
                    for u in (c, c + 1):
                        gather(u + 4)
                        scatter(i, u - 4)

            pipeline(pool, step)
            pool.wait_ge(part_in, 64)
            for q in range(4):
                cs = slice(2 * q, 2 * q + 2)
                pool.wait_ge(fin_in1[q], 16)
                if q >= 2:
                    pool.wait_ge(sh_added, q - 1)
                pool.tensor_tensor(part[2][:, cs, :], part[2][:, cs, :], work2[:, cs, :], ALU.add).then_inc(sum_pool, 1)
                if q >= 2:
                    pool.wait_ge(fin_in3[q], 16)
                    pool.wait_ge(sum_pool, 2 * q - 1)
                    pool.tensor_tensor(part[2][:, cs, :], part[2][:, cs, :], part[3][:, cs, :], ALU.add
                                       ).then_inc(sum_pool, 1)
            for k in range(2):
                cs = slice(2 * k, 2 * k + 2)
                pool.wait_ge(norm_act, 14 + 2 * k)
                pool.tensor_tensor(work[:, cs, :], work[:, cs, :], x_sb[:, cs, :], ALU.add).then_inc(fin_pool, 1)

        @block.scalar
        def _(act):
            def first_rsqrt(q, c0):
                act.wait_ge(var_done, q + 1)
                act.activation(rs0[:, c0:c0 + TB], ve[:, c0:c0 + TB], ACT.Abs_reciprocal_sqrt).then_inc(rs_act, 1)

            def normalise(q, dst, src, c0, first=2):
                act.wait_ge(rstd_done, q + 1)
                act.wait_ge(shift_done, q + 1)
                for c in range(c0 + first, c0 + TB):
                    act.activation(dst[:, c, :], src[:, c, :], ACT.Identity, bias=shift[:, c:c + 1],
                                   scale=rstd[:, c:c + 1]).then_inc(norm_act, 1)

            def gate_z(b):
                for m in range(2):
                    n = 2 * b + m
                    act.wait_ge(z_ps, n + 1)
                    act.activation(Z[:, m, b, :], bank[4 + n][:], ACT.Tanh, scale=0.5).then_inc(z_th, 1)
                    act.wait_ge(z_th, n + 1)
                    act.activation(Z[:, m, b, :], Z[:, m, b, :], ACT.Relu).then_inc(z_relu, 1)
                    act.wait_ge(z_relu, n + 1)
                    act.activation(sq[:, m, b, :], Z[:, m, b, :], ACT.Square, bias=half_one[:, 1:2]).then_inc(z_sq, 1)

            def first_inv(b):
                act.wait_ge(pk, b + 1)
                act.activation(inv[:, b, :], peak[:, b, :], ACT.Abs_reciprocal_sqrt).then_inc(inv_act, 1)

            def gate_r(k):
                rk = r4[:, 2 * k:2 * k + 2, :]
                act.wait_ge(r_ps, k + 1)
                act.activation(rk, bank[k][:].rearrange("p (c d) -> p c d", c=2), ACT.Tanh, scale=0.5).then_inc(r_th, 1)
                act.wait_ge(r_th, k + 1)
                act.activation(rk, rk, ACT.Relu).then_inc(r_relu, 1)
                act.wait_ge(r_relu, k + 1)
                act.activation(rk, rk, ACT.Square, scale=0.5, bias=half_one[:, 0:1]).then_inc(r_sq, 1)
                act.wait_ge(r_sq, k + 1)
                act.activation(rk, rk, ACT.Square).then_inc(r4_done, 1)

            def gate_silu(n):
                rows = SC[n % 3][1]
                act.wait_ge(gu_ps, n + 1)
                if n >= 2:
                    act.wait_ge(gu_mul, n - 1)
                act.activation(gsil[0:rows, n % 2, :], bank[2 * (n % 2)][0:rows, :], ACT.Silu).then_inc(gu_sil, 1)

            def copy_down(k):
                act.wait_ge(dn_ps, k + 1)
                act.activation(y_sh[:, 2 * k:2 * k + 2, :], dn_b[k][:].rearrange("p (c d) -> p c d", c=2),
                               ACT.Copy).then_inc(dn_cp, 1)

            first_rsqrt(0, 0)
            normalise(0, work, x_sb, 0)
            first_rsqrt(1, TB)
            for k in range(KC):
                act.wait_ge(xnT_ps, k + 1)
                act.activation(xnT[:, k, 0, 1:T + 1], bank[k][:], ACT.Copy).then_inc(xnT_act, 1)
            normalise(1, work, x_sb, TB)
            act.wait_ge(consts, 4)
            gate_z(0)
            first_inv(0)
            act.wait_ge(xnT_ps, 4)
            act.activation(xnT[:, 1, 1, 1:T + 1], bank[3][:], ACT.Copy).then_inc(xnT_act, 1)
            gate_z(1)
            first_inv(1)
            gate_r(0)
            gate_r(1)
            for b in range(B):
                first_rsqrt(2 + 2 * b, TB * b)
                normalise(2 + 2 * b, work, work, TB * b)
                first_rsqrt(3 + 2 * b, TB * b)
                normalise(3 + 2 * b, x2n, x_sb, TB * b)
                act.wait_ge(x2T_ps, 2 * b + 2)
                act.activation(x2nT[:, 1, T * b:T * b + T], x2T_b[b][1][:], ACT.Copy).then_inc(x2T_act, 1)
                if b == 0:
                    gate_r(2)
                    gate_r(3)
                    gate_silu(0)
            gate_silu(1)
            gate_silu(2)
            for h in range(2):
                cs = slice(TB * h, TB * h + TB)
                act.wait_ge(lg_sub, h + 1)
                act.activation(prob[:, cs, :], below[:, cs, 0:E], ACT.Exp).then_inc(lg_exp, 1)
            gate_silu(3)
            copy_down(0)
            copy_down(1)
            gate_silu(4)
            gate_silu(5)
            left_over = []

            def step(i, c):
                s = TURN * i + c
                if exists(i, c + 1):
                    act.wait_ge(tx_ps, s + 2)
                    if later(i, c, 1):
                        act.wait_ge(h_ps, s)
                    act.activation(xT[:, (c + 1) % 2, :, :], x_b[:, 0:C].rearrange(
                        "p (k t) -> p k t", k=KC), ACT.Copy).then_inc(xT_done, 1)
                if exists(i, c):
                    act.wait_ge(h_ps, s + 1)
                    if later(i, c, 2):
                        act.wait_ge(hT_ps, s - 1)
                    act.activation(hS[:, c % 2, :], h_b[c % 2][:, 0:I], ACT.Silu).then_inc(h_done, 1)
                if exists(i, c - 2):
                    e = s - 2
                    act.wait_ge(y_ps, e + 1)
                    if later(i, c, 10):
                        act.wait_ge(scat[acc_of(i, c - 10)], added(i, c - 10) + 16)
                    act.wait_ge(sum_done, 4 * i + (c - 2) // 4 + 1)
                    act.activation(yS[:, (c - 2) % 8, :], y_b[c % 2][:, 0:C], ACT.Copy,
                                   scale=slot_sum[:, ((c - 2) // 4) % 4, (c - 2) % 4, 1:2]).then_inc(y_done, 1)
                if isinstance(i, int) and s == LAST - 4:
                    act.wait_ge(ext_done, 1)
                    left_over.append(act.value_load(ext_i[0:1, EXTRA:EXTRA + 1], min_val=0, max_val=1))

            pipeline(act, step)
            with act.If(left_over[0]):
                with act.Fori(0, E * NT) as n:
                    act.wait_ge(o_h_ps, n + 1)
                    act.activation(hS[:, 0, :], h_b[0][:, 0:I], ACT.Silu).then_inc(o_h, 1)
            for h in range(2):
                first_rsqrt(6 + h, TB * h)
                normalise(6 + h, work, work, TB * h, first=2 * h)

        @block.tensor
        def _(pe):
            WARM = 30

            def turn(b, src, dst):
                for k in range(KC):
                    for j in range(TB):
                        mm = pe.transpose(dst[k][:, P * j:P * j + P], src[:, TB * b + j, P * k:P * k + P], ident[:])
                    yield mm

            def product_z(b):
                for m in range(2):
                    for k in range(2 * KC):
                        late = k // KC
                        mm = pe.matmul(bank[4 + 2 * b + m][:], wact_sb[:, k, m, :], xnT[:, k % KC, b, late:late + T],
                                       start=(k == 0), stop=(k == 2 * KC - 1))
                    mm.then_inc(z_ps, 1)

            def product_r(c):
                b, j = c // TB, c % TB
                for k in range(2 * KC):
                    at = P * j + k // KC
                    mm = pe.matmul(bank[c // 2][:, C * (c % 2):C * (c % 2) + C], xnT[:, k % KC, b, at:at + P],
                                   wrec_sb[:, k, :], start=(k == 0), stop=(k == 2 * KC - 1))
                if c % 2:
                    mm.then_inc(r_ps, 1)

            def product_v(b):
                for c in range(TB * b, TB * b + TB):
                    for m in range(2):
                        mm = pe.matmul(bank[4 + c // 2][:, C * (c % 2):C * (c % 2) + C],
                                       Z[:, m, b, P * (c % TB):P * (c % TB) + P], wval_sb[:, m, :],
                                       start=(m == 0), stop=(m == 1))
                    if c % 2:
                        mm.then_inc(v_ps, 1)

            def logits(b):
                for c in range(TB * b, TB * b + TB):
                    for k in range(KC):
                        mm = pe.matmul(bank[4][:, E * c:E * c + E], x2nT[:, k, P * c:P * c + P], gate_sb[:, k, :],
                                       start=(k == 0), stop=(k == KC - 1))
                mm.then_inc(lg_ps, 1)

            def down(k):
                for c in (2 * k, 2 * k + 1):
                    for j, (_, rows) in enumerate(SC):
                        w = sda_sb[:, j, :] if j < 2 else sdb_sb[:]
                        mm = pe.matmul(dn_b[k][:, C * (c % 2):C * (c % 2) + C],
                                       hidT[0:rows, j, P * c:P * c + P], w, start=(j == 0), stop=(j == 2))
                mm.then_inc(dn_ps, 1)

            def gate_up(n):
                half, (at, rows) = n // 3, SC[n % 3]
                if n == 0:
                    pe.wait_ge(w_in["sgu"], 16)
                if n >= 2:
                    pe.wait_ge(gu_mul, n - 1)
                for g in range(2):
                    for k in range(KC):
                        mm = pe.matmul(bank[2 * (n % 2) + g][0:rows, :], sgu_sb[:, k, IS * g + at:IS * g + at + rows],
                                       x2nT[:, k, T * half:T * half + T], start=(k == 0), stop=(k == KC - 1))
                mm.then_inc(gu_ps, 1)

            def tables(i, c):
                e = TURN * i + c
                pe.wait_ge(hit_done, 2 * e + 2)
                if c % 4 == 0 and later(i, c, 4):
                    pe.wait_ge(sum_done, 4 * i + c // 4)
                at = RC * (c % 4)
                for t in range(NT):
                    mm = pe.matmul(tab_b[:, at:at + RC], hit[:, c % 2, :, t], tslice[:, c % 2, t, :],
                                   start=(t == 0), stop=(t == NT - 1))
                mm.then_inc(tab_ps, 1)

            pe.wait_ge(consts, 8)
            for _ in range(WARM):
                pe.transpose(bank[7][:, 0:P], ident[:], ident[:])
            pe.wait_ge(norm_dve, 2)
            pe.wait_ge(norm_act, 2)
            for mm in turn(0, work, bank[0:2]):
                mm.then_inc(xnT_ps, 1)
            pe.wait_ge(w_in["wact"], 16)
            pe.wait_ge(xnT_act, 2)
            product_z(0)
            pe.wait_ge(norm_dve, 4)
            pe.wait_ge(norm_act, 4)
            for mm in turn(1, work, bank[2:4]):
                mm.then_inc(xnT_ps, 1)
            pe.wait_ge(xnT_dve, 1)
            pe.wait_ge(xnT_act, 3)
            product_z(1)
            pe.wait_ge(w_in["wrec"], 16)
            for c in range(5):
                product_r(c)
            pe.wait_ge(w_in["wval"], 16)
            pe.wait_ge(kv_done, 1)
            pe.wait_ge(z_th, 2)
            product_v(0)
            for c in range(5, NT):
                product_r(c)
            pe.wait_ge(r_th, 2)
            pe.wait_ge(norm_dve, 8)
            pe.wait_ge(norm_act, 8)
            for mm in turn(0, x2n, x2T_b[0]):
                mm.then_inc(x2T_ps, 1)
            pe.wait_ge(x2T_dve, 1)
            pe.wait_ge(x2T_act, 1)
            gate_up(0)
            pe.wait_ge(w_in["gate"], 16)
            pe.wait_ge(y_mul, 2)
            logits(0)
            pe.wait_ge(kv_done, 2)
            pe.wait_ge(share_done, 3)
            pe.wait_ge(z_th, 4)
            product_v(1)
            pe.wait_ge(r_th, 4)
            gate_up(1)
            gate_up(2)
            pe.wait_ge(norm_dve, 12)
            pe.wait_ge(norm_act, 12)
            pe.wait_ge(y_mul, 4)
            for mm in turn(1, x2n, x2T_b[1]):
                mm.then_inc(x2T_ps, 1)
            pe.wait_ge(x2T_dve, 2)
            pe.wait_ge(x2T_act, 2)
            pe.wait_ge(lg_sub, 1)
            logits(1)
            pe.wait_ge(w_in["sda"], 16)
            pe.wait_ge(w_in["sdb"], 16)
            gate_up(3)
            pe.wait_ge(gu_mul, 3)
            down(0)
            pe.wait_ge(mask_done, 2)
            pe.matmul(bank[6][:], tri[:], mask[:].rearrange("p c e -> p (c e)"), start=True, stop=False)
            for t in range(1, NT):
                mm = pe.matmul(bank[6][:, E * t:], ones[:], mask[:, 0:NT - t, :].rearrange("p c e -> p (c e)"),
                               start=False, stop=(t == NT - 1))
            mm.then_inc(rank_ps, 1)
            for t in range(NT):
                mm = pe.matmul(bank[7][:, 0:E], ones[:], mask[:, t, :], start=(t == 0), stop=(t == NT - 1))
            mm.then_inc(rank_ps, 1)
            down(1)
            pe.wait_ge(dn_cp, 1)
            for e in range(2):
                tables(0, e)
            pe.wait_ge(dn_cp, 2)
            gate_up(4)
            for e in range(2, 4):
                tables(0, e)
            gate_up(5)
            for e in range(4, 6):
                tables(0, e)
            for e in range(6, 8):
                tables(0, e)
            pe.wait_ge(rank_read, 2)

            def hidden(dst, xTe, w):
                for k in range(KC):
                    mm = pe.matmul(dst, xTe[:, k, :], w[:, I * k:I * k + I], start=(k == 0), stop=(k == KC - 1))
                return mm

            def turn_hidden(dst, h):
                pe.transpose(dst[:, 0:P], h[:, 0:P], ident[:])
                return pe.transpose(dst[0:IR, P:2 * P], h[:, P:I], ident[:])

            def output(dst, hTe, w, wr):
                pe.matmul(dst, hTe[:, 0, :], w[:, KC * I:KC * I + C], start=True, stop=False)
                return pe.matmul(dst, hTe[0:IR, 1, :], wr, start=False, stop=True)

            def step(i, c):
                s = TURN * i + c
                if exists(i, c + 1):
                    e, u = s + 1, c + 1
                    pe.wait_ge(gath[u % 8], 32 * i + 16 * (u // 8 + 1))
                    if later(i, c, 0):
                        pe.wait_ge(xT_done, s + 1)
                    for k in range(KC):
                        mm = pe.transpose(x_b[:, P * k:P * k + P],
                                          xg[:, u % 8, P * k:P * k + P], ident[:])
                    mm.then_inc(tx_ps, 1)
                if exists(i, c):
                    if not later(i, c, 1):
                        pe.wait_ge(gu_mul, 6)
                    if isinstance(i, int) and s >= E:
                        pe.wait_ge(wld_ext[s - E], 32)
                    else:
                        pe.wait_ge(wld[(c // 2) % 4], 64 * i + 32 * (c // 8 + 1))
                    pe.wait_ge(xT_done, s + 1)
                    if later(i, c, 2):
                        pe.wait_ge(h_done, s - 1)
                    hidden(h_b[c % 2][:, 0:I], xT[:, c % 2], w12_sb[:, c % 8]).then_inc(h_ps, 1)
                if exists(i, c - 1):
                    u = c - 1
                    pe.wait_ge(h_done, s)
                    if later(i, c, 3):
                        pe.wait_ge(hT_done, s - 2)
                    turn_hidden(hT_b[u % 2][:, 0:2 * P], hS[:, u % 2]).then_inc(hT_ps, 1)
                if exists(i, c - 2):
                    u = c - 2
                    pe.wait_ge(hT_done, s - 1)
                    if later(i, c, 4):
                        pe.wait_ge(y_done, s - 3)
                    output(y_b[u % 2][:, 0:C], hT[:, u % 2], w12_sb[:, u % 8], w2b_sb[:, u % 8, :]).then_inc(y_ps, 1)
                if has_table(i, c + 9):
                    tables(i, c + 9)

            pipeline(pe, step)
            pe.wait_ge(xT_done, NB)
            pe.wait_ge(sum_done, (NB + 3) // 4)
            down(2)
            down(3)
            pe.wait_ge(ext_done, 1)
            with pe.If(pe.value_load(ext_i[0:1, EXTRA:EXTRA + 1], min_val=0, max_val=1)):
                with pe.Fori(0, E * NT) as n:
                    pe.wait_ge(o_x, n + 1)
                    hidden(h_b[0][:, 0:I], xT[:, 0], ow12).then_inc(o_h_ps, 1)
                    pe.wait_ge(o_h, n + 1)
                    turn_hidden(hT_b[0][:, 0:2 * P], hS[:, 0]).then_inc(o_t_ps, 1)
                    pe.wait_ge(o_t, n + 1)
                    output(y_b[0][:, 0:C], hT[:, 0], ow12, ow2b).then_inc(o_y_ps, 1)

        @block.vector
        def _(dve):
            count = [0]

            def mark(ins):
                count[0] += 1
                ins.then_inc(d, 1)

            def settle():
                dve.wait_ge(d, count[0])

            def link(ins):
                mark(ins)
                settle()

            def stats_of(src, cs):
                for c in cs:
                    mark(dve.bn_stats(stats[:, c, :], src[:, c, :]))
                settle()
                for c in cs:
                    mark(dve.bn_aggr(mv[:, c, :], stats[:, c, :]))

            def variances(c0):
                settle()
                cs = slice(c0, c0 + TB)
                dve.tensor_scalar(ve[:, cs], mv[:, cs, 1], EPS, None, ALU.add).then_inc(var_done, 1)

            def sharpen(q, c0):
                cs = slice(c0, c0 + TB)
                dve.wait_ge(rs_act, q + 1)
                link(dve.scalar_tensor_tensor(nt0[:, cs], rs0[:, cs], -0.5, rs0[:, cs], ALU.mult, ALU.mult))
                link(dve.tensor_tensor(nt1[:, cs], nt0[:, cs], ve[:, cs], ALU.mult))
                dve.scalar_tensor_tensor(rstd[:, cs], nt1[:, cs], 1.5, rs0[:, cs], ALU.add, ALU.mult
                                         ).then_inc(rstd_done, 1)
                dve.wait_ge(rstd_done, q + 1)
                dve.scalar_tensor_tensor(shift[:, cs], mv[:, cs, 0], -1.0, rstd[:, cs], ALU.mult, ALU.mult
                                         ).then_inc(shift_done, 1)

            def normalise(q, dst, src, c0):
                for c in (c0, c0 + 1):
                    dve.tensor_scalar(dst[:, c, :], src[:, c, :], mv[:, c, 0:1], rstd[:, c:c + 1],
                                      ALU.subtract, ALU.mult).then_inc(norm_dve, 1)

            for b in range(B):
                for k in (2 * b, 2 * b + 1):
                    dve.wait_ge(x_in[k], 16)
                    stats_of(x_sb, (2 * k, 2 * k + 1))
                variances(TB * b)
                sharpen(b, TB * b)
                normalise(b, work, x_sb, TB * b)
            dve.wait_ge(xnT_ps, 3)
            dve.tensor_copy(xnT[:, 0, 1, 1:T + 1], bank[2][:]).then_inc(xnT_dve, 1)

            def running_max(b):
                dve.wait_ge(mag_done, b + 1)
                dve.tensor_tensor_scan(peak[:, b, :], mag2[:, b, :], mag2[:, b, :], 0.0, ALU.max, ALU.max).then_inc(pk, 1)

            def multiply(hi, lo, room):
                n = hi.shape[2]
                pr, pi = room
                mark(dve.tensor_tensor(pr, lo[:, 0:1].to_broadcast([P, 2, n]), hi, ALU.mult))
                link(dve.tensor_tensor(pi, lo[:, 1:2].to_broadcast([P, 2, n]), hi[:, ::-1], ALU.mult))
                mark(dve.tensor_tensor(hi[:, 0], pr[:, 0], pi[:, 0], ALU.subtract))
                link(dve.tensor_tensor(hi[:, 1], pr[:, 1], pi[:, 1], ALU.add))

            def level(b, first, end, dist):
                multiply(*factors(b, first, end, dist, prod))

            def scan_blocks(b):
                step = 2 * UP[-1]
                dist = step
                while dist < T:
                    multiply(Z[:, :, b, step - 1 + dist:T:step], Z[:, :, b, step - 1:T - dist:step],
                             parts(prod, (T - dist) // step))
                    dist *= 2

            def gate_up(n):
                half, rows = n // 3, SC[n % 3][1]
                dve.wait_ge(gu_sil, n + 1)
                dve.tensor_tensor(hidT[0:rows, n % 3, T * half:T * half + T], gsil[0:rows, n % 2, :],
                                  bank[2 * (n % 2) + 1][0:rows, :], ALU.mult).then_inc(gu_mul, 1)

            def residual(b):
                c0 = TB * b
                for k in range(2 * b, 2 * b + 2):
                    dve.wait_ge(v_ps, k + 1)
                    dve.wait_ge(r4_done, k + 1)
                    dve.tensor_tensor(work[:, 2 * k:2 * k + 2, :], bank[4 + k][:].rearrange("p (c d) -> p c d", c=2),
                                      r4[:, 2 * k:2 * k + 2, :], ALU.mult).then_inc(y_mul, 1)
                    dve.wait_ge(y_mul, k + 1)
                    stats_of(work, (2 * k, 2 * k + 1))
                variances(c0)
                sharpen(2 + 2 * b, c0)
                normalise(2 + 2 * b, work, work, c0)
                for done, cs in ((norm_dve, slice(c0, c0 + 2)), (norm_act, slice(c0 + 2, c0 + 4))):
                    dve.wait_ge(done, 2 * (3 + 2 * b))
                    link(dve.tensor_tensor(x_sb[:, cs, :], x_sb[:, cs, :], work[:, cs, :], ALU.add))
                    stats_of(x_sb, (cs.start, cs.start + 1))
                variances(c0)
                sharpen(3 + 2 * b, c0)
                normalise(3 + 2 * b, x2n, x_sb, c0)

            def columns(b):
                dve.wait_ge(x2T_ps, 2 * b + 1)
                dve.tensor_copy(x2nT[:, 0, T * b:T * b + T], x2T_b[b][0][:]).then_inc(x2T_dve, 1)

            lg = bank[4][:].rearrange("p (c e) -> p c e", c=NT)
            tb = table[:, 0:E, :, :].rearrange("p e c n -> p c e n")

            def below_max(h):
                cs = slice(TB * h, TB * h + TB)
                dve.wait_ge(lg_ps, h + 1)
                link(dve.tensor_reduce(lmax[:, cs], lg[:, cs, :], AX.X, ALU.max))
                dve.wait_ge(consts, 17)
                dve.tensor_tensor(below[:, cs, 0:E], lg[:, cs, :], lmax[:, cs].unsqueeze(2).to_broadcast([P, TB, E]),
                                  ALU.subtract).then_inc(lg_sub, 1)

            def choose(h):
                cs = range(TB * h, TB * h + TB)
                dve.wait_ge(lg_sub, h + 1)
                for c in cs:
                    mark(dve.max(top8[:, c, :], below[:, c, :]))
                settle()
                for c in cs:
                    mark(dve.match_replace(left[:, c, :], top8[:, c, :], below[:, c, :], 4.0))
                settle()
                dve.tensor_scalar(mask[:, cs.start:cs.stop, :], left[:, cs.start:cs.stop, 0:E], 3.0, None, ALU.is_gt
                                  ).then_inc(mask_done, 1)

            def weigh(h):
                cs = slice(TB * h, TB * h + TB)
                dve.wait_ge(mask_done, h + 1)
                dve.wait_ge(lg_exp, h + 1)
                link(dve.tensor_tensor(cw[:, cs, :], prob[:, cs, :], mask[:, cs, :], ALU.mult))
                link(dve.tensor_reduce(wsum[:, cs], cw[:, cs, :], AX.X, ALU.add))
                link(dve.reciprocal(wnorm[:, cs], wsum[:, cs]))
                link(dve.tensor_tensor(cw[:, cs, :], cw[:, cs, :], wnorm[:, cs].unsqueeze(2).to_broadcast([P, TB, E]),
                                       ALU.mult))
                link(dve.tensor_copy(tb[:, cs, :, 3], cw[:, cs, :]))
                link(dve.tensor_tensor(left[:, cs, 0:E], cw[:, cs, :], tb[:, cs, :, 3], ALU.subtract))
                link(dve.tensor_copy(tb[:, cs, :, 4], left[:, cs, 0:E]))
                link(dve.tensor_tensor(tb[:, cs, :, 5], left[:, cs, 0:E], tb[:, cs, :, 4], ALU.subtract))

            dve.wait_ge(z_sq, 2)
            dve.tensor_tensor(mag2[:, 0, :], sq[:, 0, 0, :], sq[:, 1, 0, :], ALU.add).then_inc(mag_done, 1)
            running_max(0)
            dve.tensor_scalar(Z[:, :, 0, CUT:], Z[:, :, 0, CUT:], 1.0, None, ALU.add).then_inc(z_plus, 1)
            dve.wait_ge(inv_act, 1)
            dve.wait_ge(pk, 1)
            m, v = mag2[:, 0, 0:CUT], inv[:, 0, 0:CUT]
            link(dve.scalar_tensor_tensor(m, v, -0.5, v, ALU.mult, ALU.mult))
            link(dve.tensor_tensor(m, m, peak[:, 0, 0:CUT], ALU.mult))
            link(dve.scalar_tensor_tensor(v, m, 1.5, v, ALU.add, ALU.mult))
            for m in range(2):
                mark(dve.scalar_tensor_tensor(Z[:, m, 0, 0:CUT], Z[:, m, 0, 0:CUT], 1.0, v, ALU.add, ALU.mult))
            settle()
            for dist in UP:
                level(0, 2 * dist - 1, CUT, dist)
            dve.wait_ge(share_done, 1)
            scan_blocks(0)
            dve.wait_ge(z_sq, 4)
            dve.tensor_scalar(Z[:, :, 1, :], Z[:, :, 1, :], 1.0, None, ALU.add).then_inc(z_plus, 1)
            running_max(1)
            for dist in UP[::-1]:
                level(0, 3 * dist - 1, T, dist)
            dve.tensor_copy(nt0[:, 0:1], nt0[:, 0:1]).then_inc(kv_done, 1)
            residual(0)
            columns(0)
            dve.wait_ge(share_done, 2)
            scan_blocks(1)
            dve.tensor_copy(nt0[:, 0:1], nt0[:, 0:1]).then_inc(blocks_done, 1)
            for dist in UP[::-1]:
                level(1, 3 * dist - 1, CUT, dist)
            dve.tensor_copy(nt0[:, 0:1], nt0[:, 0:1]).then_inc(kv_done, 1)
            gate_up(0)
            residual(1)
            below_max(0)
            columns(1)
            choose(0)
            gate_up(1)
            gate_up(2)
            weigh(0)
            below_max(1)
            choose(1)
            weigh(1)
            gate_up(3)
            dve.wait_ge(rank_ps, 1)
            link(dve.scalar_tensor_tensor(rank1[:, 0:E, :].rearrange("p e c -> p c e"),
                                          bank[6][:].rearrange("p (c e) -> p c e", c=NT), 1.0, mask[:],
                                          ALU.add, ALU.mult))
            link(dve.tensor_scalar(table[:, 0:E, :, 2], rank1[:, 0:E, :], -1.0, 1.0, ALU.mult, ALU.add))

            def hits(i, c):
                e = TURN * i + c
                if later(i, c, 2):
                    dve.wait_ge(tab_ps, e - 1)
                dve.tensor_tensor(hit[:, c % 2], rank1[:, bass.ds(e, 1), :].to_broadcast([P, SLOTS, NT]), slot_no[:],
                                  ALU.is_equal).then_inc(hit_done, 1)
                dve.tensor_copy(tslice[:, c % 2], table[:, bass.ds(e, 1)].rearrange("p e c n -> p (e c) n")
                                ).then_inc(hit_done, 1)

            def sums(i, c):
                e, r = TURN * i + c, (c // 4) % 4
                dve.wait_ge(tab_ps, e + 1)
                if later(i, c, 16):
                    dve.wait_ge(tx_ps, e - 15)
                    dve.wait_ge(y_done, e - 15)
                    for u in range(c - c % 4 - 16, c - c % 4 - 12):
                        dve.wait_ge(scat[acc_of(i, u)], added(i, u) + 16)
                dve.tensor_reduce(slot_sum[:, r], tab_b[:, 0:4 * RC].rearrange(
                    "p (e q n) -> p e q n", e=4, q=2), AX.X, ALU.add).then_inc(sum_done, 1)
                dve.wait_ge(sum_done, 4 * i + c // 4 + 1)
                dve.tensor_scalar(gat_idx[:, r], slot_sum[:, r, :, 0], trash_no[:, 0:1], None, ALU.add
                                  ).then_inc(idx_done, 1)

            for e in range(4):
                hits(0, e)
            gate_up(4)
            sums(0, 3)
            for e in range(4, 6):
                hits(0, e)
            dve.scalar_tensor_tensor(rank_f[:], bank[6][:].rearrange("p (c e) -> p c e", c=NT), 1.0, mask[:],
                                     ALU.add, ALU.mult).then_inc(rank_read, 1)
            dve.wait_ge(rank_ps, 2)
            dve.tensor_scalar(full_i[:], bank[7][:, 0:E], float(SLOTS - 1), None, ALU.add).then_inc(rank_read, 1)
            for e in range(6, 8):
                hits(0, e)
            gate_up(5)
            sums(0, 7)
            left_over = []

            shape = [P, EXTRA, E]
            before_b, upto_b = before[:].unsqueeze(1).to_broadcast(shape), upto[:].unsqueeze(1).to_broadcast(shape)

            def count_blocks():
                dve.wait_ge(rank_read, 2)
                link(dve.tensor_scalar(full_i[:], full_i[:], 7, None, ALU.arith_shift_right))
                link(dve.tensor_scalar(full[:], full_i[:], -1.0, 0.0, ALU.add, ALU.max))
                link(dve.tensor_tensor_scan(upto[:], full[:], zeros[:, 0:E], 0.0, ALU.add, ALU.add))
                link(dve.tensor_tensor(before[:], upto[:], full[:], ALU.subtract))

            def find_experts():
                mark(dve.tensor_tensor(ext_a[:], before_b, ext_no[:], ALU.is_le))
                link(dve.tensor_tensor(ext_b[:], upto_b, ext_no[:], ALU.is_gt))
                link(dve.tensor_tensor(ext_a[:], ext_a[:], ext_b[:], ALU.mult))
                link(dve.tensor_tensor(ext_b[:], ext_a[:], ext_e[:], ALU.mult))
                link(dve.tensor_reduce(ext_s[:, 0, :], ext_b[:], AX.X, ALU.add))

            def find_slots():
                link(dve.scalar_tensor_tensor(ext_b[:], before_b, float(NT), ext_no[:], ALU.add, ALU.subtract))
                link(dve.tensor_tensor(ext_b[:], ext_a[:], ext_b[:], ALU.mult))
                link(dve.tensor_reduce(ext_s[:, 1, :], ext_b[:], AX.X, ALU.add))
                link(dve.tensor_scalar(ext_s[:, 1, :], ext_s[:, 1, :], float(SLOTS), -float(NTOK + SLOTS),
                                       ALU.mult, ALU.add))

            def publish():
                mark(dve.tensor_copy(ext_i[:, 0:EXTRA], ext_s[:, 0, :]))
                link(dve.tensor_scalar(ext_i[:, EXTRA:], upto[:, E - 1:E], float(EXTRA), None, ALU.is_gt))
                dve.tensor_copy(nt0[:, 0:1], ext_s[:, 0, 0:1]).then_inc(ext_done, 1)

            def fill_block(n):
                e = dve.value_load(ext_i[0:1, n:n + 1], min_val=0, max_val=E - 1)
                mark(dve.tensor_scalar(rank1[:, E + n:E + n + 1, :], rank_f[:, :, bass.ds(e, 1)].rearrange("p c e -> p e c"),
                                       ext_s[:, 1, n:n + 1], None, ALU.add))
                link(dve.tensor_copy(table[:, E + n:E + n + 1], table[:, bass.ds(e, 1)]))
                link(dve.tensor_scalar(table[:, E + n, :, 2], rank1[:, E + n, :], -1.0, 1.0, ALU.mult, ALU.add))

            assert EXTRA == 2

            def step(i, c):
                s = TURN * i + c
                if has_table(i, c + 9):
                    hits(i, c + 9)
                if exists(i, c - 1):
                    dve.wait_ge(hT_ps, s)
                    if later(i, c, 3):
                        dve.wait_ge(y_ps, s - 2)
                    u = (c - 1) % 2
                    dve.tensor_copy(hT[:, u].rearrange("p k t -> p (k t)"), hT_b[u][:, 0:2 * P]
                                    ).then_inc(hT_done, 1)
                if later(i, c, 0) and has_table(i, c + 8) and (c % 4 == 3 or not has_table(i, c + 9)):
                    sums(i, c + 8)
                if isinstance(i, int):
                    if s == 3:
                        count_blocks()
                    elif s == 4:
                        find_experts()
                    elif s == 5:
                        find_slots()
                    elif s == 6:
                        publish()
                    elif s in (7, 8):
                        fill_block(s - 7)
                    elif s == LAST - 4:
                        left_over.append(dve.value_load(ext_i[0:1, EXTRA:EXTRA + 1], min_val=0, max_val=1))

            pipeline(dve, step)

            with dve.If(left_over[0]):
                for q in range(4):
                    dve.wait_ge(fin_in[q], 16)
                block_i = left[:, :, 0:E].bitcast(I32)
                dve.tensor_scalar(block_i, rank_f[:], float(SLOTS - 1), None, ALU.add).then_inc(o_cw, 1)
                dve.wait_ge(o_cw, 1)
                dve.tensor_scalar(block_i, block_i, 7, None, ALU.arith_shift_right).then_inc(o_cw, 1)
                dve.wait_ge(o_cw, 2)
                dve.tensor_copy(rank_f[:], block_i).then_inc(o_cw, 1)
                dve.wait_ge(o_cw, 3)
                dve.scalar_tensor_tensor(cw[:], rank_f[:], 1.5, cw[:], ALU.is_gt, ALU.mult).then_inc(o_cw, 1)
                dve.wait_ge(o_cw, 4)
                dve.tensor_tensor(rank_f[:], rank_f[:], before[:].unsqueeze(1).to_broadcast([P, NT, E]),
                                  ALU.add).then_inc(o_cw, 1)
                dve.wait_ge(o_cw, 5)
                dve.scalar_tensor_tensor(over_cw, rank_f[:], EXTRA + 1.5, cw[:], ALU.is_gt, ALU.mult).then_inc(o_y, 1)
                with dve.Fori(0, E) as e:
                    dve.wait_ge(o_y, e * NT + 1)
                    dve.wait_ge(o_ld, 32 * e + 32)
                    for c in range(NT):
                        n = e * NT + c
                        dve.tensor_copy(xT[:, 0], x2nT[:, :, P * c:P * c + P]).then_inc(o_x, 1)
                        dve.wait_ge(o_t_ps, n + 1)
                        dve.tensor_copy(hT[:, 0].rearrange("p k t -> p (k t)"), hT_b[0][:, 0:2 * P]).then_inc(o_t, 1)
                        dve.wait_ge(o_y_ps, n + 1)
                        dve.scalar_tensor_tensor(work[:, c, :], y_b[0][:, 0:C], over_cw[:, c, bass.ds(e, 1)],
                                                 work[:, c, :], ALU.mult, ALU.add).then_inc(o_y, 1)
                dve.wait_ge(o_y, E * NT + 1)

            dve.wait_ge(part_in, 64)
            for k in (2, 3):
                cs = slice(2 * k, 2 * k + 2)
                dve.wait_ge(dn_ps, k + 1)
                dve.tensor_tensor(part[2][:, cs, :], part[2][:, cs, :], dn_b[k][:].rearrange("p (c d) -> p c d", c=2),
                                  ALU.add).then_inc(sh_added, 1)
            for q in range(4):
                cs = slice(2 * q, 2 * q + 2)
                dve.wait_ge(fin_in[q], 16)
                if q < 2:
                    dve.wait_ge(fin_in3[q], 16)
                    link(dve.tensor_tensor(work[:, cs, :], work[:, cs, :], part[3][:, cs, :], ALU.add))
                dve.wait_ge(sum_pool, (1, 2, 4, 6)[q])
                link(dve.tensor_tensor(work[:, cs, :], work[:, cs, :], part[2][:, cs, :], ALU.add))
                stats_of(work, (2 * q, 2 * q + 1))
                if q == 1:
                    variances(0)
                elif q == 2:
                    sharpen(6, 0)
            variances(TB)
            sharpen(7, TB)
            normalise(7, work, work, TB)
            for k in (2, 3):
                cs = slice(2 * k, 2 * k + 2)
                dve.wait_ge((norm_dve, norm_act)[k - 2], (14, 18)[k - 2])
                dve.tensor_tensor(work[:, cs, :], work[:, cs, :], x_sb[:, cs, :], ALU.add).then_inc(fin_dve, 1)


def kernel(L0_attn_x, L0_attn_W_act, L0_attn_W_val, L0_attn_W_rec, L0_ffn_gate_w, L0_ffn_experts_w1,
           L0_ffn_experts_w2, L0_ffn_shared_gate_up, L0_ffn_shared_down):
    import numpy as np
    import concourse.bacc as bacc
    from concourse.bass_utils import run_bass_kernel_spmd

    x = np.asarray(L0_attn_x)
    bx, tx, C = x.shape
    KC = C // P
    E, I, _ = L0_ffn_experts_w1.shape
    IS = L0_ffn_shared_down.shape[1]

    def by_k(w):
        w = np.asarray(w)
        return w.T.reshape(w.shape[1] // P, P, w.shape[0]).transpose(1, 0, 2)

    w_act = by_k(L0_attn_W_act).reshape(P, 2 * KC, C // 2, 2).transpose(0, 1, 3, 2)
    w_val = np.asarray(L0_attn_W_val).T.reshape(C // 2, 2, C)
    w1 = np.asarray(L0_ffn_experts_w1).transpose(0, 2, 1).reshape(E, KC, P, I).transpose(0, 2, 1, 3).reshape(E, P, KC * I)
    w2 = np.asarray(L0_ffn_experts_w2).transpose(0, 2, 1)
    sd = np.asarray(L0_ffn_shared_down).T
    arrays = {
        "x": x.reshape(bx * tx, C),
        "w_act": w_act,
        "w_rec": by_k(L0_attn_W_rec),
        "w_val": w_val,
        "gate": by_k(L0_ffn_gate_w),
        "w12": np.concatenate([w1, w2[:, 0:P, :]], axis=2),
        "w2b": w2[:, P:, :],
        "sgu": by_k(L0_ffn_shared_gate_up),
        "sd_a": sd[0:2 * P].reshape(2, P, C).transpose(1, 0, 2),
        "sd_b": sd[2 * P:],
    }
    arrays = {n: np.ascontiguousarray(a) for n, a in arrays.items()}
    nc = bacc.Bacc("TRN2", target_bir_lowering=False, num_devices=1)
    aps = {n: nc.dram_tensor(n, a.shape, F32, kind="ExternalInput").ap() for n, a in arrays.items()}
    out = nc.dram_tensor("out", (bx * tx, C), F32, kind="ExternalOutput").ap()
    moe_block(nc, out=out, **aps)
    r = run_bass_kernel_spmd(nc, [arrays], core_ids=[0])
    return r.results[0]["out"].reshape(bx, tx, C)
```
